# Optimizing a Trainium2 kernel written in Bass

```python
import numpy as np
import jax
import jax.numpy as jnp

def _softmax(x, axis=-1):
    return jax.nn.softmax(x, axis=axis)
def _gelu(x):
    return jax.nn.gelu(x, approximate=True)
def _silu(x):
    return jax.nn.silu(x)
def _sigmoid(x):
    return jax.nn.sigmoid(x)
def _layernorm(x, axis=-1, eps=1e-5):
    m = jnp.mean(x, axis=axis, keepdims=True)
    v = jnp.var(x, axis=axis, keepdims=True)
    return (x - m) / jnp.sqrt(v + eps)
def _scatter_add(tgt, idx, src, axis=0):
    return tgt.at[idx].add(src)
def _segment_sum(src, seg, n):
    return jax.ops.segment_sum(src, seg, n)

kernel_name = 'mk_adj_resnorm_d1_adj_512_09e870'

def setup_inputs(seed: int = 0):
    np.random.seed(seed)
    _w = jnp.asarray
    def _rec_inputs():
        import jax
        import jax.numpy as jnp
        _gk = jax.random.key(seed)
        x = -0.0005963 + 1.001 * jax.random.normal(jax.random.fold_in(_gk, 1), (6144, 512), jnp.float32)
        _a = jax.random.bernoulli(jax.random.fold_in(_gk, 2), 0.00260417, (6144, 6144))
        _a = jnp.logical_or(_a, jnp.swapaxes(_a, -1, -2))
        _a = jnp.logical_or(_a, jnp.eye(6144, dtype=bool))
        adj = _a.astype(jnp.int32)
        return x, adj
    x, adj = _rec_inputs()
    def _L0_gnn_setup():
        import jax, jax.numpy as jnp
        import numpy as np
        N = 6144
        IN_FEATS = 512
        OUT_FEATS = 64
        NHEADS = 8
        ALPHA = 0.2
        NEG_BIG = -9000000000000000.0
        key = jax.random.key(seed)
        k_x, k_adj, k_w, k_a1, k_a2 = jax.random.split(key, 5)
        x = jax.random.normal(k_x, (N, IN_FEATS), dtype=jnp.float32)
        adj = jax.random.randint(k_adj, (N, N), 0, 2, dtype=jnp.int32)
        gain = 1.414
        bw = gain * np.sqrt(6.0 / (IN_FEATS + OUT_FEATS))
        W = jax.random.uniform(k_w, (NHEADS, IN_FEATS, OUT_FEATS), jnp.float32, -bw, bw)
        ba = gain * np.sqrt(6.0 / (OUT_FEATS + 1))
        a1 = jax.random.uniform(k_a1, (NHEADS, OUT_FEATS), jnp.float32, -ba, ba)
        a2 = jax.random.uniform(k_a2, (NHEADS, OUT_FEATS), jnp.float32, -ba, ba)
        return {'x': x, 'adj': adj, 'W': W, 'a1': a1, 'a2': a2}
    _L0_gnn_all = _L0_gnn_setup()
    _L0_gnn_in = {k: v for k, v in _L0_gnn_all.items() if k in ('W', 'a1', 'a2', )}
    del _L0_gnn_all

    return {
        "x": x,
        "adj": adj,
        "L0_gnn_W": _L0_gnn_in["W"],
        "L0_gnn_a1": _L0_gnn_in["a1"],
        "L0_gnn_a2": _L0_gnn_in["a2"],
    }

def reference(x, adj, L0_gnn_W, L0_gnn_a1, L0_gnn_a2):
    import jax
    import jax.numpy as jnp
    def _L0_gnn_ref(x, adj, W, a1, a2):
        import jax, jax.numpy as jnp
        import numpy as np
        N = 6144
        IN_FEATS = 512
        OUT_FEATS = 64
        NHEADS = 8
        ALPHA = 0.2
        NEG_BIG = -9000000000000000.0
        h = jnp.einsum('ni,hif->hnf', x, W)
        s1 = jnp.einsum('hnf,hf->hn', h, a1)
        s2 = jnp.einsum('hnf,hf->hn', h, a2)
        scores = jax.nn.leaky_relu(s1[:, :, None] + s2[:, None, :], negative_slope=ALPHA)
        scores = jnp.where(adj[None] > 0, scores, NEG_BIG)
        att = jax.nn.softmax(scores, axis=-1)
        out = jnp.einsum('hnm,hmf->hnf', att, h)
        out = jnp.transpose(out, (1, 0, 2)).reshape(N, NHEADS * OUT_FEATS)
        return jax.nn.elu(out)

    x = _layernorm(x + _L0_gnn_ref(x, adj, L0_gnn_W, L0_gnn_a1, L0_gnn_a2), axis=-1)
    return x


_drawn_inputs = setup_inputs


def setup_inputs(seed=0):
    import zlib

    import numpy as np

    out = dict(_drawn_inputs(seed))
    spreads = {}
    factors = {}
    for name, (base, spread) in spreads.items():
        noise = np.random.default_rng([zlib.crc32(name.encode()), seed]).standard_normal(out[name].shape)
        drawn = base * np.exp(spread * noise) if base else spread * noise
        out[name] = jnp.asarray(drawn.astype(out[name].dtype))
    for name, factor in factors.items():
        out[name] = (out[name] * factor).astype(out[name].dtype)
    return out
```

```python
from contextlib import ExitStack

import concourse.bass as bass
from concourse import mybir

P = 128
F32, F16, BF16, F8 = mybir.dt.float32, mybir.dt.float16, mybir.dt.bfloat16, mybir.dt.float8e4
I32, I8, U8 = mybir.dt.int32, mybir.dt.int8, mybir.dt.uint8
ALU, ACT, AX = mybir.AluOpType, mybir.ActivationFunctionType, mybir.AxisListType
RMAX = bass.bass_isa.ReduceOp.max

ONE_F8 = 0x38
SLOPE = 0.2
EPS = 1e-5
VSCALE = 512.0
LEAST = 2.0 ** -22
LO = 2048.0
IBT = 8
SEG = 8
RING = 4
PAIR = 2


def bass_gat(nc, x, adj, W, a1, a2, out):
    N, K = x.shape
    NH, _, D = W.shape
    NT = N // P
    KC = K // P
    IB = IBT * P
    NB = N // IB
    NG = NH // 2
    NPAIR = NT // PAIR
    NSEG = NT // SEG
    PPS = SEG // PAIR
    D1 = D + 1
    REG = 2 * D1
    PER_BANK = 512 // REG
    NACC = 2 * IBT
    NBANK = -(-NACC // PER_BANK)
    XPB = NBANK

    def acc_of(sg, t):
        return sg * IBT + t

    assert NBANK + 2 <= 8 and PPS == RING and NT % SEG == 0 and N % IB == 0

    adjt_d = nc.dram_tensor("adjt_scratch", [NB * NT // PAIR, P, PAIR, IB], U8, kind="Internal").ap()
    h_d = nc.dram_tensor("h_scratch", [N, NH * D], F32, kind="Internal").ap()
    s1_d = nc.dram_tensor("negs1_scratch", [NH * NT, P], F32, kind="Internal").ap()
    att_d = nc.dram_tensor("att_scratch", [N, NH * D1], F32, kind="Internal").ap()

    ctx = ExitStack()
    with ctx:
        def sb(name, shape, dt):
            return ctx.enter_context(nc.sbuf_tensor(name, shape, dt))

        def sem(name):
            return ctx.enter_context(nc.semaphore(name))

        ps = ctx.enter_context(nc.psum_tensor("ps", [P, 8, 512], F32))

        ADJB = NT * IB
        VB = 2 * NT * 2 * REG * 2
        big = sb("big", [P, ADJB + VB], U8)
        adjt = big[:, 0:ADJB].rearrange("p (c i) -> p c i", c=NT)
        V = big[:, ADJB:ADJB + VB].bitcast(F16).rearrange("p (h c s r) -> p h c s r", h=2, c=NT, s=2)
        y_all = big[:, 0:NT * K * 4].bitcast(F32).rearrange("p (t f) -> p t f", t=NT)

        adj_in = sb("adj_in", [P, 2, IBT, PAIR * P], I32)
        adj_bf = sb("adj_bf", [P, 2, IBT, PAIR * P], BF16)
        adj_u8 = sb("adj_u8", [P, 4, IB], U8)
        s1b = sb("s1b", [P, 2, IB], F32)
        cmp = sb("cmp", [P, RING, PAIR * IB], I8)
        pos = sb("pos", [P, RING, PAIR * IB], U8)
        neg = sb("neg", [P, RING, PAIR * IB], U8)
        raw = sb("raw", [P, NACC * REG], F32)
        comb = sb("comb", [P, NACC * D1], F32)
        num = sb("num", [P, IBT * D1], F32)
        hseg = sb("hseg", [P, 2, SEG, D1], F32)
        vtmp = sb("vtmp", [P, 2, SEG * D1], F32)
        ltmp = sb("ltmp", [P, 2, SEG * D1], F32)
        sc = sb("sc", [P, 2 * NH, NT], F32)
        negs = sb("negs", [P, 2 * NH, NT], F32)
        bd = sb("bd", [P, 2, NH, NT], F32)
        ac = sb("ac", [P, NH, 2, NT], F32)
        t1 = sb("t1", [P, NH, NT], F32)
        t2 = sb("t2", [P, NH, NT], F32)
        t3 = sb("t3", [P, NH, NT], F32)
        u = sb("u", [P, NH, NT], F32)
        cmax = sb("cmax", [P, NH], F32)
        call = sb("call", [P, NH], F32)
        hmax = sb("hmax", [P, NT], F32)
        hm = sb("hm", [P, 2], F32)
        mv2 = sb("mv2", [P, 2, 2], F32)
        okt = sb("okt", [P, NT, NH], F32)
        id32 = sb("id32", [P, P], F32)
        id16 = sb("id16", [P, P], BF16)
        zero16 = sb("zero16", [P, P], F16)
        s1r = sb("s1r", [P, NH * NT], F32)
        stats = sb("stats", [P, 2, 6], F32)
        mv = sb("mv", [P, NT, 2], F32)
        rstd = sb("rstd", [P, NT], F32)
        epsc = sb("epsc", [P, 1], F32)
        rstd2 = sb("rstd2", [P, NT], F32)
        frec = sb("frec", [P, 2, NH], F32)
        xs = cmp[:, :, :].rearrange("p a b -> p (a b)").bitcast(F32).rearrange("p (a f) -> p a f", f=K)
        hsb = pos[:, :, :].rearrange("p a b -> p (a b)").bitcast(F32).rearrange("p (a f) -> p a f", f=K)
        xT = neg[:, :, :].rearrange("p a b -> p (a b)").bitcast(F32).rearrange("p (a f) -> p a f", f=K)
        junk = big[:, ADJB + 24 * 1024:ADJB + 26 * 1024 + 0].bitcast(F32)
        hsegd = raw[:, 0:2 * SEG * D1].rearrange("p (a c f) -> p a c f", a=2, c=SEG)
        vtmpd = raw[:, 2 * SEG * D1:3 * SEG * D1]
        ltmpd = raw[:, 3 * SEG * D1:4 * SEG * D1]
        fin = adj_in[:, :, :, :].rearrange("p a t j -> p (a t j)").bitcast(F32)
        fatt = fin[:, 0:2 * NH * D1].rearrange("p (a h f) -> p a h f", a=2, h=NH)
        fx = fin[:, 2 * NH * D1:2 * NH * D1 + 2 * K].rearrange("p (a f) -> p a f", a=2)
        fv = cmp[:, :, :].rearrange("p a b -> p (a b)").bitcast(F32)[:, 0:2 * K].rearrange("p (a f) -> p a f", a=2)
        fr = pos[:, :, :].rearrange("p a b -> p (a b)").bitcast(F32)[:, 0:2 * K].rearrange("p (a f) -> p a f", a=2)
        fn = pos[:, :, :].rearrange("p a b -> p (a b)").bitcast(F32)[:, 2 * K:4 * K].rearrange("p (a f) -> p a f", a=2)
        fe = neg[:, :, :].rearrange("p a b -> p (a b)").bitcast(F32)[:, 0:2 * K].rearrange("p (a f) -> p a f", a=2)
        fw = neg[:, :, :].rearrange("p a b -> p (a b)").bitcast(F32)[:, 2 * K:4 * K].rearrange("p (a f) -> p a f", a=2)
        Wsb = big[:, ADJB:ADJB + KC * K * 4].bitcast(F32).rearrange("p (c n) -> p c n", c=KC)
        o_w = ADJB + KC * K * 4
        Wa = big[:, o_w:o_w + KC * 2 * NH * 4].bitcast(F32).rearrange("p (c n) -> p c n", c=KC)
        o_w += KC * 2 * NH * 4
        av = big[:, o_w:o_w + 2 * K * 4].bitcast(F32).rearrange("p (s n) -> p s n", s=2)
        o_w += 2 * K * 4
        wprod = big[:, o_w:o_w + 2 * KC * K * 4].bitcast(F32).rearrange("p (s c n) -> p s c n", s=2, c=KC)

        w_loaded = sem("w_loaded")
        ident_made = sem("ident_made")
        wa_step = sem("wa_step")
        x_loaded = [sem("x_loaded0"), sem("x_loaded1")]
        x_turned = sem("x_turned")
        xt_ready = sem("xt_ready")
        h_ready = sem("h_ready")
        h_copied = sem("h_copied")
        h_stored = [sem("h_stored0"), sem("h_stored1")]
        h_maxed = sem("h_maxed")
        h_sq = sem("h_sq")
        f_aggr = sem("f_aggr")
        c_part = sem("c_part")
        c_all = sem("c_all")
        tab_dve = sem("tab_dve")
        tab_act = sem("tab_act")
        s1_turned = sem("s1_turned")
        s1_stored = sem("s1_stored")
        adj_loaded = [sem("adj_loaded0"), sem("adj_loaded1")]
        adj_cast = sem("adj_cast")
        adj_turned = sem("adj_turned")
        adj_evac = sem("adj_evac")
        adj_stored = [sem("adj_stored0"), sem("adj_stored1")]
        adjt_loaded = sem("adjt_loaded")
        s1b_loaded = [sem("s1b_loaded0"), sem("s1b_loaded1")]
        cmp_act = sem("cmp_act")
        cmp_dve = sem("cmp_dve")
        pos_done = sem("pos_done")
        neg_done = sem("neg_done")
        pair_used = sem("pair_used")
        evac_act = sem("evac_act")
        evac_dve = sem("evac_dve")
        comb_step = sem("comb_step")
        raw_used = sem("raw_used")
        att_stored = sem("att_stored")
        hd_loaded = [sem("hd_loaded0"), sem("hd_loaded1")]
        hp_loaded = [sem("hp_loaded0"), sem("hp_loaded1")]
        vstep_dve = sem("vstep_dve")
        vstep_pool = sem("vstep_pool")
        v_built = [sem("v_built0"), sem("v_built1")]
        fatt_loaded = [sem("fatt_loaded0"), sem("fatt_loaded1")]
        fx_loaded = [sem("fx_loaded0"), sem("fx_loaded1")]
        f_rec = sem("f_rec")
        f_val = sem("f_val")
        f_relu = sem("f_relu")
        f_exp = sem("f_exp")
        f_elu = sem("f_elu")
        f_sum = sem("f_sum")
        f_bn = sem("f_bn")
        f_var = sem("f_var")
        f_std = sem("f_std")
        f_rstd = sem("f_rstd")
        f_out = sem("f_out")
        out_stored = sem("out_stored")

        passed_pe, passed_dve, passed_pool, passed_sp = (
            sem(f"passed_{e}") for e in ("pe", "dve", "pool", "sp"))

        C_TURNED, C_HREADY, C_HCOP, C_MAX, C_CAST, C_CHUNK, C_EV = 2, 2, 2, 2, 2, 2, 2
        C_RING, C_BANK, C_FIN = RING, NBANK // 2, 2

        adj_r = adj.rearrange("(b t p) j -> b p t j", t=IBT, p=P)
        x_r = x.rearrange("(t p) f -> t p f", p=P)
        out_r = out.rearrange("(t p) f -> t p f", p=P)
        att_r = att_d.rearrange("(t p) (h f) -> t p h f", p=P, h=NH)
        att_b = att_d.rearrange("(b t p) (h f) -> b h p t f", t=IBT, p=P, h=NH)
        h_r = h_d.rearrange("(t p) f -> t p f", p=P)
        h_s = h_d.rearrange("(s c p) (h f) -> s h p c f", c=SEG, p=P, h=NH)
        s1_rows = s1_d.rearrange("(h b t) p -> (h b) (t p)", h=NH, t=IBT)
        adjt_s = adjt_d.rearrange("(s m) p a i -> s p m (a i)", m=PPS)
        adjt32 = big[:, 0:ADJB].bitcast(I32)
        pos32, neg32, cmp32 = (a[:, :, :].bitcast(I32) for a in (pos, neg, cmp))
        pos8, neg8 = pos[:, :, :].bitcast(F8), neg[:, :, :].bitcast(F8)
        W32 = PAIR * IB // 4
        ACT_ONLY = {False: (0, 2), True: (0,)}
        DVE_CMP = {k: PPS - len(v) for k, v in ACT_ONLY.items()}

        block = ctx.enter_context(nc.Block())

        @block.sync
        def _(sp):
            def load_unit(b, k, i):
                sp.wait_ge(adj_cast, b * NPAIR + k + 1 - 2 + C_CAST)
                sp.dma_start(adj_in[:, i], adj_r[b, :, :, bass.ds(k * (PAIR * P), PAIR * P)]
                             ).then_inc(adj_loaded[i], 16)

            def load_adjt(n, b, s, used):
                sp.wait_ge(neg_done, used)
                for e in range(2):
                    sp.wait_ge(adj_stored[e], (b * (NPAIR // 2) + (s + 1) * (PPS // 2)) * 16)
                sp.wait_ge(adjt_loaded, n * 16)
                sp.sem_inc(passed_sp, 1)
                sp.dma_start(adjt[:, s * SEG:(s + 1) * SEG, :].rearrange("p (m a) i -> p m (a i)", a=PAIR),
                             adjt_s[b * NSEG + s]).then_inc(adjt_loaded, 16)

            def load_s1(head, b, hd, used):
                sp.wait_ge(cmp_act, used)
                sp.sem_inc(passed_sp, 1)
                sp.wait_ge(pos_done, used + C_RING)
                sp.sem_inc(passed_sp, 1)
                sp.dma_start(s1b[:, hd], s1_rows[head * NB + b].partition_broadcast(P)
                             ).then_inc(s1b_loaded[hd], 16)

            for c in range(KC):
                sp.dma_start(Wsb[:, c].rearrange("p (h f) -> p h f", h=NH),
                             W[:, c * P:(c + 1) * P, :].rearrange("h p f -> p h f")).then_inc(w_loaded, 16)
            for s, a in enumerate((a1, a2)):
                sp.dma_start(av[:, s], a.rearrange("h f -> (h f)").partition_broadcast(P)).then_inc(w_loaded, 16)

            with sp.Fori(0, NT // 4) as i:
                for j in range(4):
                    sp.wait_ge(x_turned, i * 4 + j + 1 - 2 + C_TURNED)
                    sp.dma_start(xs[:, j % 2], x_r[i * 4 + j]).then_inc(x_loaded[j % 2], 16)
                    if j % 2:
                        load_unit(0, i * 2 + j // 2, j // 2)

            for e in range(2):
                sp.wait_ge(h_stored[e], NT // 2 * 16)
            sp.wait_ge(ident_made, 1)
            for s in range(NSEG):
                if s >= 2:
                    sp.wait_ge(vstep_dve, 8 * (s - 1))
                sp.dma_start(hsegd[:, s % 2, :, 0:D], h_s[s, 0]).then_inc(hd_loaded[s % 2], 16)
                if s == 1:
                    sp.wait_ge(s1_stored, 16)
                    load_s1(0, 0, 0, 0)
                if s < NSEG - 2:
                    load_adjt(s, 0, s, 0)

            def iteration(g, b, nxt, T, produce):
                for s in range(NSEG):
                    if produce:
                        for i in range(2):
                            load_unit(b + 1, 2 * s + i, i)
                    if s == 1:
                        load_s1(g * 2 + 1, b, 1, T * (2 * NPAIR))
                    if s < 2:
                        load_adjt(T * NSEG + NSEG - 2 + s, b, NSEG - 2 + s, T * (2 * NPAIR))
                for s in range(NSEG):
                    if produce:
                        for i in range(2):
                            load_unit(b + 1, NPAIR // 2 + 2 * s + i, i)
                    if nxt and s == 1:
                        load_s1(nxt[0] * 2, nxt[1], 0, T * (2 * NPAIR) + NPAIR)
                    if nxt and s >= 2:
                        load_adjt((T + 1) * NSEG + s - 2, nxt[1], s - 2,
                                  T * (2 * NPAIR) + NPAIR + PPS * (s - 1))

            with sp.Fori(0, NB - 1) as b:
                iteration(0, b, (0, b + 1), b, True)
            iteration(0, NB - 1, (1, 0), NB - 1, False)
            with sp.Fori(1, NG - 1) as g:
                with sp.Fori(0, NB - 1) as b:
                    iteration(g, b, (g, b + 1), g * NB + b, False)
                iteration(g, NB - 1, (g + 1, 0), g * NB + NB - 1, False)
            with sp.Fori(0, NB - 1) as b:
                iteration(NG - 1, b, (NG - 1, b + 1), (NG - 1) * NB + b, False)
            iteration(NG - 1, NB - 1, None, NG * NB - 1, False)

            sp.wait_ge(att_stored, 16 * 2 * NG * NB)
            with sp.Fori(0, NT // 2) as i:
                for j in range(2):
                    sp.wait_ge(f_val, i * 2 + j + 1 - 2 + C_FIN)
                    sp.wait_ge(f_sum, i * 2 + j + 1 - 2 + C_FIN)
                    sp.dma_start(fatt[:, j], att_r[i * 2 + j]).then_inc(fatt_loaded[j], 16)
                    sp.dma_start(fx[:, j], x_r[i * 2 + j]).then_inc(fx_loaded[j], 16)
            with sp.Fori(0, NT) as t:
                sp.wait_ge(f_out, t + 1)
                sp.dma_start(out_r[t], y_all[:, t, :]).then_inc(out_stored, 16)
            sp.wait_ge(out_stored, 16 * NT)

        @block.scalar
        def _(act):
            def evac_chunk(c4, q):
                act.wait_ge(adj_turned, c4 * 4 + q + 1 + C_CHUNK)
                if q % 2 == 0:
                    act.wait_ge(adj_stored[q // 2], c4 * 16)
                act.copy(adj_u8[:, q], ps[:, XPB + q % 2].bitcast(BF16)).then_inc(adj_evac, 1)
                if q % 2:
                    act.wait_ge(adj_evac, c4 * 4 + q + 1 + C_EV)
                    act.dma_start(adjt_d[c4 * 2 + q // 2], adj_u8[:, q - 1:q + 1]
                                  ).then_inc(adj_stored[q // 2], 16)

            def stage1(i, evacs):
                for q in range(4):
                    t, j = i * 4 + q, q % 2
                    act.wait_ge(h_ready, t + 1 + C_HREADY)
                    act.wait_ge(h_stored[j], (i * 2 + q // 2) * 16)
                    act.wait_ge(h_maxed, t + 1 - 2 + C_MAX)
                    act.copy(sc[:, :, t], ps[:, 4 + j, 0:2 * NH])
                    act.copy(hsb[:, j], ps[:, 2 + j]).then_inc(h_copied, 1)
                    act.wait_ge(h_copied, t + 1 + C_HCOP)
                    act.dma_start(h_r[t], hsb[:, j]).then_inc(h_stored[j], 16)
                    if q < evacs:
                        evac_chunk(i, q)

            with act.Fori(0, NT // 4 - 1) as i:
                stage1(i, 4)
            stage1(NT // 4 - 1, 2)

            act.wait_ge(tab_dve, 1)
            act.activation(bd[:, 0], t1[:, :, :], ACT.Exp).then_inc(tab_act, 1)
            act.activation(bd[:, 1], t1[:, :, :], ACT.Exp, scale=SLOPE).then_inc(tab_act, 1)
            act.wait_ge(tab_dve, 3)
            act.activation(ac[:, :, 0, :], t2[:, :, :], ACT.Exp).then_inc(tab_act, 1)
            act.activation(ac[:, :, 1, :], t3[:, :, :], ACT.Exp).then_inc(tab_act, 1)
            act.wait_ge(tab_dve, 4)

            def evac_banks(H):
                act.wait_ge(pair_used, (H + 1) * NPAIR + C_RING)
                act.wait_ge(raw_used, H)
                for n in range(0, NBANK, 2):
                    w = min(PER_BANK, NACC - n * PER_BANK) * REG
                    act.copy(raw[:, n * PER_BANK * REG:n * PER_BANK * REG + w], ps[:, n, 0:w]
                             ).then_inc(evac_act, 1)

            def segment(g, hd, T, s, produce, after=None):
                for q in range(PPS):
                    pair = (T * 2 + hd) * NPAIR + s * PPS + q
                    act.wait_ge(pos_done, pair + 1 - RING + C_RING)
                    for c in range(PAIR):
                        if c == 0 or q in ACT_ONLY[produce]:
                            i = act.activation(
                                cmp[:, q, c * IB:(c + 1) * IB], s1b[:, hd], ACT.Sign,
                                bias=negs[:, NH + g * 2 + hd, bass.ds(s * SEG + q * PAIR + c, 1)])
                    i.then_inc(cmp_act, 1)
                    if after:
                        after(s, q)

            def head(g, hd, T, produce, flush=False, first=False):
                act.wait_ge(s1b_loaded[hd], T * 16 + 16)
                n4 = T * (NPAIR // 2) + hd * NSEG + NT // 4 - 1

                def after(s, q):
                    if produce or (flush and hd == 0 and q < 2):
                        evac_chunk(n4 + s + (2 + q) // 4, (2 + q) % 4)

                def after_first(s, q):
                    after(s, q)
                    if q == (1 if produce else 2) and not first:
                        evac_banks(T * 2 + hd - 1)
                segment(g, hd, T, 0, produce, after_first)
                with act.Fori(1, NSEG) as s:
                    segment(g, hd, T, s, produce, after if produce else None)

            head(0, 0, 0, True, first=True)
            head(0, 1, 0, True)
            with act.Fori(1, NB - 1) as b:
                for hd in range(2):
                    head(0, hd, b, True)
            for hd in range(2):
                head(0, hd, NB - 1, False, flush=True)
            with act.Fori(1, NG) as g:
                with act.Fori(0, NB) as b:
                    for hd in range(2):
                        head(g, hd, g * NB + b, False)
            evac_banks(2 * NG * NB - 1)

            def elu_parts(i, j):
                t = i * 2 + j
                act.wait_ge(f_val, t + 1 + C_FIN)
                act.wait_ge(f_elu, t + 1 - 2 + C_FIN)
                act.activation(fn[:, j], fv[:, j], ACT.Relu, scale=-1.0).then_inc(f_relu, 1)
                act.activation(fr[:, j], fv[:, j], ACT.Relu)
                act.wait_ge(f_relu, t + 1)
                act.activation(fe[:, j], fn[:, j], ACT.Exp, scale=-1.0).then_inc(f_exp, 1)

            with act.Fori(0, NT // 2) as i:
                for j in range(2):
                    elu_parts(i, j)
            act.wait_ge(f_var, NT)
            act.wait_ge(ident_made, 1)
            act.activation(rstd[:, :], mv[:, :, 1], ACT.Sqrt, bias=epsc[:, 0:1]).then_inc(f_std, 1)

        @block.vector
        def _(dve):
            dve.sem_inc(adj_cast, C_CAST)
            dve.sem_inc(h_maxed, C_MAX)
            dve.sem_inc(pos_done, C_RING)
            dve.sem_inc(evac_dve, C_BANK)
            for f in (f_val, f_exp, f_elu, f_sum):
                dve.sem_inc(f, C_FIN)

            dve.wait_ge(w_loaded, 16 * (KC + 2))
            for s in range(2):
                dve.tensor_tensor(wprod[:, s], Wsb, av[:, s:s + 1, :].to_broadcast([P, KC, NH * D]),
                                  ALU.mult).then_inc(wa_step, 1)
            for s in range(2):
                dve.wait_ge(wa_step, s + 1)
                dve.tensor_reduce(Wa[:, :, s * NH:(s + 1) * NH],
                                  wprod[:, s].rearrange("p c (h f) -> p c h f", h=NH), AX.X, ALU.add
                                  ).then_inc(wa_step, 1)

            def cast_unit(b, k, half, i):
                un = b * NPAIR + k
                dve.wait_ge(adj_loaded[i], half * 16 + 16)
                dve.wait_ge(adj_turned, un * 2 - 2 + C_CHUNK)
                dve.tensor_scalar(adj_bf[:, i], adj_in[:, i], 0.0, float(ONE_F8), ALU.is_gt, ALU.mult
                                  ).then_inc(adj_cast, 1)

            with dve.Fori(0, NT // 4) as i:
                for q in range(4):
                    t, j = i * 4 + q, q % 2
                    dve.wait_ge(x_turned, t + 1 + C_TURNED)
                    dve.wait_ge(h_ready, t + 1 - 2 + C_HREADY)
                    dve.tensor_copy(xT[:, j], ps[:, j]).then_inc(xt_ready, 1)
                    if q % 2 == 0:
                        cast_unit(0, i * 2 + q // 2, i, q // 2)
                    dve.wait_ge(h_copied, t + 1 + C_HCOP)
                    dve.wait_ge(h_maxed, t + C_MAX)
                    dve.sem_inc(passed_dve, 1)
                    dve.tensor_tensor_reduce(junk, hsb[:, j], hsb[:, j], 1.0, 0.0, ALU.mult, ALU.max,
                                             hm[:, j:j + 1]).then_inc(h_sq, 1)
                    dve.wait_ge(h_sq, t + 1)
                    dve.tensor_copy(hmax[:, bass.ds(t, 1)], hm[:, j:j + 1]).then_inc(h_maxed, 1)

            dve.wait_ge(h_copied, NT + C_HCOP)
            dve.tensor_reduce(cmax[:, :], sc[:, NH:2 * NH, :], AX.X, ALU.max).then_inc(c_part, 1)
            dve.wait_ge(c_all, 1)
            call_b = call[:, :].unsqueeze(2).to_broadcast([P, NH, NT])
            dve.tensor_tensor(t1[:, :, :], sc[:, NH:2 * NH, :], call_b, ALU.subtract).then_inc(tab_dve, 1)
            dve.tensor_tensor(u[:, :, :], sc[:, 0:NH, :], call_b, ALU.add).then_inc(vstep_dve, 1)
            dve.wait_ge(vstep_dve, 1)
            dve.tensor_scalar(t2[:, :, :], u[:, :, :], 1.0 - SLOPE, 0.0, ALU.mult, ALU.min).then_inc(tab_dve, 1)
            dve.tensor_scalar(t3[:, :, :], u[:, :, :], SLOPE - 1.0, 0.0, ALU.mult, ALU.min).then_inc(tab_dve, 1)
            dve.tensor_scalar(negs[:, :, :], sc[:, :, :], -1.0, None, ALU.mult).then_inc(tab_dve, 1)
            dve.wait_ge(tab_act, 2)
            dve.tensor_scalar(bd[:, :, :, :], bd[:, :, :, :], VSCALE, None, ALU.mult).then_inc(tab_dve, 1)
            dve.wait_ge(s1_turned, 1)
            dve.tensor_copy(s1r[:, :], ps[:, 0, 0:NH * NT]).then_inc(tab_dve, 1)

            def build(eng, step, base, hseg_, v_, l_, hd, s, head, done):
                for sg in range(2):
                    k = base + sg * 4
                    fac = bd[:, sg, head, s * SEG:(s + 1) * SEG].unsqueeze(2).to_broadcast([P, SEG, D1])
                    v3, l3 = (a.rearrange("p (c f) -> p c f", c=SEG) for a in (v_, l_))
                    dst = V[:, hd, s * SEG:(s + 1) * SEG, sg]
                    eng.wait_ge(step, k)
                    eng.tensor_tensor(v3, hseg_, fac, ALU.mult).then_inc(step, 1)
                    eng.wait_ge(step, k + 1)
                    eng.tensor_copy(dst[:, :, 0:D1], v3).then_inc(step, 1)
                    eng.wait_ge(step, k + 2)
                    eng.tensor_tensor(l3, v3, dst[:, :, 0:D1], ALU.subtract).then_inc(step, 1)
                    eng.wait_ge(step, k + 3)
                    i = eng.tensor_scalar(dst[:, :, D1:REG], l3, LO, None, ALU.mult)
                    i.then_inc(step, 1)
                eng.wait_ge(step, base + 8)
                eng.sem_inc(done, 1)

            dve.wait_ge(tab_dve, 5)
            dve.wait_ge(h_maxed, NT + C_MAX)
            dve.wait_ge(h_ready, NT + C_HREADY)
            for s in range(NSEG):
                dve.wait_ge(hd_loaded[s % 2], s // 2 * 16 + 16)
                build(dve, vstep_dve, 8 * s + 1, hsegd[:, s % 2], vtmpd, ltmpd, 0, s, 0, v_built[0])

            def evac_bank(n, H):
                dve.wait_ge(raw_used, H)
                w = min(PER_BANK, NACC - n * PER_BANK) * REG
                dve.tensor_copy(raw[:, n * PER_BANK * REG:n * PER_BANK * REG + w], ps[:, n, 0:w]
                                ).then_inc(evac_dve, 1)

            def evac_banks(H):
                dve.wait_ge(pair_used, (H + 1) * NPAIR + C_RING)
                for n in range(1, NBANK, 2):
                    evac_bank(n, H)

            def segment(g, hd, T, s, produce, b=None, evac=None):
                base = (T * 2 + hd) * NPAIR + s * PPS
                n = 0
                for q in range(PPS):
                    pair = base + q
                    if evac is not None and q == PPS - 1:
                        evac_banks(evac)
                    if q not in ACT_ONLY[produce]:
                        dve.wait_ge(pos_done, pair + 1 - RING + C_RING)
                        dve.tensor_scalar(cmp[:, q, IB:2 * IB], s1b[:, hd],
                                          sc[:, NH + g * 2 + hd, bass.ds(s * SEG + q * PAIR + 1, 1)],
                                          -1.0, ALU.is_lt, ALU.mult).then_inc(cmp_dve, 1)
                        n += 1
                        n4 = (T * 2 + hd) * NSEG + s
                        past = 0 if produce else (NB - 1) * 2 * NSEG * (DVE_CMP[True] - DVE_CMP[False])
                        dve.wait_ge(cmp_dve, n4 * DVE_CMP[produce] + past + n)
                    dve.wait_ge(cmp_act, pair + 1)
                    dve.wait_ge(pair_used, pair + 1 - RING + C_RING)
                    a = adjt32[:, bass.ds((s * PPS + q) * W32, W32)]
                    dve.tensor_tensor(pos32[:, q], cmp32[:, q], a, ALU.bitwise_and).then_inc(pos_done, 1)
                    dve.wait_ge(pos_done, pair + 1 + C_RING)
                    dve.tensor_tensor(neg32[:, q], pos32[:, q], a, ALU.bitwise_xor).then_inc(neg_done, 1)
                    if produce and q % 2 == 0:
                        cast_unit(b + 1, hd * (NPAIR // 2) + s * 2 + q // 2,
                                  (b + 1) * (NPAIR // 2) + hd * (NPAIR // 4) + s, q // 2)

            def head(g, hd, T, produce, b=None, first=False):
                dve.wait_ge(s1b_loaded[hd], T * 16 + 16)
                if hd == 0:
                    dve.wait_ge(adjt_loaded, T * (16 * NSEG) + 16)
                segment(g, hd, T, 0, produce, b, None if first else T * 2 + hd - 1)
                with dve.Fori(1, NSEG) as s:
                    if hd == 0:
                        dve.wait_ge(adjt_loaded, (T * NSEG + s) * 16 + 16)
                    segment(g, hd, T, s, produce, b)

            head(0, 0, 0, True, 0, first=True)
            head(0, 1, 0, True, 0)
            with dve.Fori(1, NB - 1) as b:
                for hd in range(2):
                    head(0, hd, b, True, b)
            for hd in range(2):
                head(0, hd, NB - 1, False)
            with dve.Fori(1, NG) as g:
                with dve.Fori(0, NB) as b:
                    for hd in range(2):
                        head(g, hd, g * NB + b, False)
            evac_banks(2 * NG * NB - 1)

            def values(i, j):
                t = i * 2 + j
                dve.wait_ge(fatt_loaded[j], i * 16 + 16)
                dve.tensor_scalar(okt[:, bass.ds(t, 1), :].rearrange("p a h -> p (a h)"), fatt[:, j, :, D],
                                  VSCALE * LEAST, None, ALU.is_ge)
                dve.reciprocal(frec[:, j], fatt[:, j, :, D]).then_inc(f_rec, 1)
                dve.wait_ge(f_rec, t + 1)
                dve.wait_ge(f_exp, t + 1 - 2 + C_FIN)
                dve.tensor_tensor(fv[:, j].rearrange("p (h f) -> p h f", h=NH), fatt[:, j, :, 0:D],
                                  frec[:, j].unsqueeze(2).to_broadcast([P, NH, D]), ALU.mult
                                  ).then_inc(f_val, 1)

            def elu(i, j):
                t = i * 2 + j
                dve.wait_ge(f_exp, t + 1 + C_FIN)
                dve.wait_ge(f_sum, t + 1 - 2 + C_FIN)
                dve.scalar_tensor_tensor(fw[:, j], fe[:, j], -1.0, fr[:, j], ALU.add, ALU.add
                                         ).then_inc(f_elu, 1)

            dve.wait_ge(neg_done, 2 * NG * NB * NPAIR)
            with dve.Fori(0, NT // 2) as i:
                for j in range(2):
                    values(i, j)
                for j in range(2):
                    elu(i, j)
            with dve.Fori(0, NT // 2) as i:
                for j in range(2):
                    t = i * 2 + j
                    dve.wait_ge(f_sum, t + 1 + C_FIN)
                    dve.wait_ge(f_var, t)
                    dve.bn_stats(stats[:, j], y_all[:, t, :]).then_inc(f_bn, 1)
                    dve.wait_ge(f_bn, t + 1)
                    dve.sem_inc(passed_dve, 1)
                    dve.bn_aggr(mv2[:, j], stats[:, j]).then_inc(f_aggr, 1)
                    dve.wait_ge(f_aggr, t + 1)
                    dve.tensor_copy(mv[:, t, :], mv2[:, j]).then_inc(f_var, 1)
            dve.wait_ge(f_std, 1)
            dve.reciprocal(rstd2[:, :], rstd[:, :]).then_inc(f_rstd, 1)
            dve.wait_ge(f_rstd, 1)
            with dve.Fori(0, NT) as t:
                dve.tensor_scalar(y_all[:, t, :], y_all[:, t, :], mv[:, t, 0:1], rstd2[:, bass.ds(t, 1)],
                                  ALU.subtract, ALU.mult).then_inc(f_out, 1)

        @block.tensor
        def _(pe):
            pe.sem_inc(x_turned, C_TURNED)
            pe.sem_inc(h_ready, C_HREADY)
            pe.sem_inc(adj_turned, C_CHUNK)
            pe.sem_inc(pair_used, C_RING)
            pe.wait_ge(ident_made, 1)

            def turn_adj(u, chunk, q):
                pe.wait_ge(adj_cast, u + 1 + C_CAST)
                pe.wait_ge(adj_evac, chunk + 1 - 2 + C_EV)
                pst = ps[:, XPB + q % 2].bitcast(BF16)
                for t in range(IBT):
                    i = pe.transpose(pst[:, t * P:(t + 1) * P],
                                     adj_bf[:, q // 2, t, q % 2 * P:(q % 2 + 1) * P], id16[:, :])
                i.then_inc(adj_turned, 1)

            def tile_h(t, j):
                pe.wait_ge(xt_ready, t + 1)
                pe.wait_ge(h_copied, t + 1 - 2 + C_HCOP)
                for c in range(KC):
                    pe.matmul(ps[:, 2 + j], xT[:, j, c * P:(c + 1) * P], Wsb[:, c], start=(c == 0),
                              stop=(c == KC - 1))
                for c in range(KC):
                    i = pe.matmul(ps[:, 4 + j, 0:2 * NH], xT[:, j, c * P:(c + 1) * P], Wa[:, c],
                                  start=(c == 0), stop=(c == KC - 1))
                i.then_inc(h_ready, 1)

            pe.wait_ge(wa_step, 4)
            with pe.Fori(0, NT // 4) as i:
                for q in range(0, 4, 2):
                    for j in range(2):
                        t = i * 4 + q + j
                        pe.wait_ge(x_loaded[j], (i * 2 + q // 2) * 16 + 16)
                        pe.wait_ge(h_ready, t + 1 - 2 + C_HREADY)
                        for c in range(KC):
                            n = pe.transpose(ps[:, j, c * P:(c + 1) * P], xs[:, j, c * P:(c + 1) * P], id32[:, :])
                        n.then_inc(x_turned, 1)
                    for j in range(2):
                        turn_adj(i * 2 + q // 2, i * 4 + q + j, q + j)
                    for j in range(2):
                        tile_h(i * 4 + q + j, j)

            pe.wait_ge(tab_dve, 4)
            pe.wait_ge(xt_ready, NT)
            n1 = negs[:, 0:NH, :].rearrange("p h t -> p (h t)")
            for c in range(NH * NT // P):
                i = pe.transpose(ps[:, 0, c * P:(c + 1) * P], n1[:, c * P:(c + 1) * P], id32[:, :])
            i.then_inc(s1_turned, 1)
            pe.wait_ge(tab_dve, 6)
            pe.wait_ge(h_copied, NT + C_HCOP)

            def block_sums(g, T, produce, b=None):
                for hd in range(2):
                    H = T * 2 + hd
                    for k in range(NPAIR):
                        q = k % RING
                        if k % PPS == 0:
                            pe.wait_ge(v_built[hd], g * NSEG + k // PPS + 1)
                        for c in range(PAIR):
                            for sg, masks, done, credit in ((0, pos8, pos_done, C_RING), (1, neg8, neg_done, 0)):
                                if c == 0:
                                    pe.wait_ge(done, H * NPAIR + k + 1 + credit)
                                    pe.sem_inc(passed_pe, 1)
                                for t in range(IBT):
                                    r = acc_of(sg, t)
                                    bank, off = r // PER_BANK, r % PER_BANK * REG
                                    if k == 0 and c == 0 and r % PER_BANK == 0:
                                        ev = evac_dve if bank % 2 else evac_act
                                        pe.wait_ge(ev, H * C_BANK - C_BANK + bank // 2 + 1 + C_BANK)
                                        pe.matmul(ps[:, bank, 0:2], zero16[:, :], zero16[:, 0:2], start=True,
                                                  stop=False, skip_group_check=True)
                                    i = pe.matmul(ps[:, bank, off:off + REG],
                                                  masks[:, q, c * IB + t * P:c * IB + (t + 1) * P],
                                                  V[:, hd, k * PAIR + c, sg, :], start=False,
                                                  stop=(k == NPAIR - 1 and c == PAIR - 1),
                                                  skip_group_check=True)
                        i.then_inc(pair_used, 1)
                        if produce:
                            turn_adj((b + 1) * NPAIR + hd * (NPAIR // 2) + k // 2,
                                     (b + 1) * NT + hd * NPAIR + k, k % 4)

            with pe.Fori(0, NB - 1) as b:
                block_sums(0, b, True, b)
            block_sums(0, NB - 1, False)
            with pe.Fori(1, NG) as g:
                with pe.Fori(0, NB) as b:
                    block_sums(g, g * NB + b, False)

        @block.gpsimd
        def _(pool):
            pool.sem_inc(h_copied, C_HCOP)
            pool.sem_inc(adj_evac, C_EV)
            pool.sem_inc(evac_act, C_BANK)
            for m in (id32, id16):
                pool.memset(m[:, :], 0.0).then_inc(comb_step, 1)
            pool.wait_ge(comb_step, 2)
            for m in (id32, id16):
                pool.affine_select(out=m[:, :], in_=m[:, :], compare_op=ALU.not_equal, fill=1.0, base=0,
                                   pattern=[[-1, P]], channel_multiplier=1).then_inc(comb_step, 1)
            pool.memset(zero16[:, :], 0.0).then_inc(comb_step, 1)
            pool.memset(epsc[:, :], EPS).then_inc(comb_step, 1)
            pool.memset(hseg[:, :, :, D:D1], 1.0).then_inc(comb_step, 1)
            pool.memset(hsegd[:, :, :, D:D1], 1.0).then_inc(comb_step, 1)
            pool.wait_ge(comb_step, 8)
            pool.sem_inc(ident_made, 1)

            pool.wait_ge(c_part, 1)
            pool.partition_all_reduce(call[:, :], cmax[:, :], P, RMAX).then_inc(c_all, 1)
            pool.wait_ge(tab_dve, 6)
            pool.dma_start(s1_d.rearrange("(q r) p -> r q p", r=P),
                           s1r[:, :].rearrange("p (q r) -> p q r", r=P)).then_inc(s1_stored, 16)

            def build(n, hd, g, free):
                head = g * 2 + hd
                for s in range(NSEG):
                    m = n * NSEG + s
                    i = s % 2
                    pool.wait_ge(vstep_pool, 8 * (m - 1) if s or not isinstance(n, int) or n else 0)
                    pool.dma_start(hseg[:, i, :, 0:D], h_s[s, head]).then_inc(hp_loaded[i], 16)
                    if free is not None:
                        pool.wait_ge(pair_used, free + PPS * (s + 1) + C_RING)
                    pool.wait_ge(hp_loaded[i], n * (NSEG // 2) * 16 + s // 2 * 16 + 16)
                    for sg in range(2):
                        k = m * 8 + sg * 4
                        fac = bd[:, sg, head, s * SEG:(s + 1) * SEG].unsqueeze(2).to_broadcast([P, SEG, D1])
                        v3 = vtmp[:, sg].rearrange("p (c f) -> p c f", c=SEG)
                        l3 = ltmp[:, sg].rearrange("p (c f) -> p c f", c=SEG)
                        dst = V[:, hd, s * SEG:(s + 1) * SEG, sg]
                        pool.wait_ge(vstep_pool, k)
                        pool.tensor_tensor(v3, hseg[:, i], fac, ALU.mult).then_inc(vstep_pool, 1)
                        pool.wait_ge(vstep_pool, k + 1)
                        pool.sem_inc(passed_pool, 1)
                        pool.tensor_copy(dst[:, :, 0:D1], v3).then_inc(vstep_pool, 1)
                        pool.wait_ge(vstep_pool, k + 2)
                        pool.tensor_tensor(l3, v3, dst[:, :, 0:D1], ALU.subtract).then_inc(vstep_pool, 1)
                        pool.wait_ge(vstep_pool, k + 3)
                        pool.sem_inc(passed_pool, 1)
                        pool.tensor_scalar(dst[:, :, D1:REG], l3, LO, 1.0, ALU.mult, ALU.mult
                                           ).then_inc(vstep_pool, 1)
                    pool.wait_ge(vstep_pool, m * 8 + 8)
                    pool.sem_inc(v_built[hd], 1)

            def combine(g, hd, b, T):
                H = T * 2 + hd
                head = g * 2 + hd
                st = 8 + H * 4
                pool.wait_ge(evac_act, H * C_BANK + C_BANK + C_BANK)
                pool.wait_ge(evac_dve, H * C_BANK + C_BANK + C_BANK)
                r3 = raw[:, :].rearrange("p (r f) -> p r f", r=NACC)
                c3 = comb[:, :].rearrange("p (r f) -> p r f", r=NACC)
                pool.wait_ge(comb_step, st)
                pool.sem_inc(passed_pool, 1)
                pool.tensor_scalar(c3, r3[:, :, D1:REG], 1.0 / LO, 1.0, ALU.mult, ALU.mult).then_inc(comb_step, 1)
                pool.wait_ge(comb_step, st + 1)
                pool.tensor_tensor(c3, c3, r3[:, :, 0:D1], ALU.add).then_inc(comb_step, 1)
                pool.wait_ge(comb_step, st + 2)
                pool.sem_inc(raw_used, 1)
                fac = ac[:, head, :, bass.ds(b * IBT, IBT)].unsqueeze(3).to_broadcast([P, 2, IBT, D1])
                c4 = comb[:, :].rearrange("p (s t f) -> p s t f", s=2, f=D1)
                pool.tensor_tensor(c4, c4, fac, ALU.mult).then_inc(comb_step, 1)
                pool.wait_ge(comb_step, st + 3)
                pool.wait_ge(att_stored, H * 16)
                pool.tensor_tensor(num[:, :].rearrange("p (t f) -> p t f", t=IBT), c4[:, 0], c4[:, 1],
                                   ALU.add).then_inc(comb_step, 1)
                pool.wait_ge(comb_step, st + 4)
                pool.dma_start(att_b[b, head], num[:, :].rearrange("p (t f) -> p t f", t=IBT)
                               ).then_inc(att_stored, 16)

            pool.wait_ge(tab_dve, 5)
            for e in range(2):
                pool.wait_ge(h_stored[e], NT // 2 * 16)
            pool.wait_ge(h_ready, NT + C_HREADY)
            pool.wait_ge(h_maxed, NT + C_MAX)
            build(0, 1, 0, None)
            pool.wait_ge(tab_act, 4)

            def group(g):
                with pool.Fori(0, NB - 1) as b:
                    for hd in range(2):
                        combine(g, hd, b, g * NB + b)
                T = g * NB + NB - 1
                for hd in range(2):
                    build(g * 2 + 1 + hd, hd, g + 1, (T * 2 + hd) * NPAIR)
                    combine(g, hd, NB - 1, T)

            with pool.Fori(0, NG - 1) as g:
                group(g)
            with pool.Fori(0, NB) as b:
                for hd in range(2):
                    combine(NG - 1, hd, b, (NG - 1) * NB + b)

            pool.wait_ge(pair_used, 2 * NG * NB * NPAIR + C_RING)
            pool.wait_ge(neg_done, 2 * NG * NB * NPAIR)
            with pool.Fori(0, NT // 2) as i:
                for j in range(2):
                    pool.wait_ge(f_elu, i * 2 + j + 1 + C_FIN)
                    pool.wait_ge(fx_loaded[j], i * 16 + 16)
                    pool.tensor_tensor(y_all[:, i * 2 + j, :], fw[:, j], fx[:, j], ALU.add).then_inc(f_sum, 1)


_INS = ['x', 'adj', 'L0_gnn_W', 'L0_gnn_a1', 'L0_gnn_a2']
_OUTS = [((6144, 512), 'float32')]


def kernel(**inputs):
    import numpy as _np
    import concourse.bacc as _bacc
    from concourse import mybir as _mybir
    from concourse.bass_utils import run_bass_kernel_spmd as _run

    nc = _bacc.Bacc("TRN2", target_bir_lowering=False, num_devices=1)
    arrays, args = {}, []
    for name in _INS:
        a = _np.ascontiguousarray(inputs[name])
        arrays[f"in_{name}_dram"] = a
        args.append(nc.dram_tensor(f"in_{name}_dram", a.shape, _mybir.dt.from_np(a.dtype), kind="ExternalInput").ap())
    for i, (shape, dtype) in enumerate(_OUTS):
        dt = _mybir.dt.from_np(_np.dtype(dtype))
        args.append(nc.dram_tensor(f"out_{i}_dram", shape, dt, kind="ExternalOutput").ap())
    bass_gat(nc, *args)
    r = _run(nc, [arrays], core_ids=[0])
    got = tuple(r.results[0][f"out_{i}_dram"] for i in range(len(_OUTS)))
    return got[0]
```

```python
from contextlib import ExitStack

import concourse.bass as bass
from concourse import mybir

P = 128
F32, F16, BF16, F8 = mybir.dt.float32, mybir.dt.float16, mybir.dt.bfloat16, mybir.dt.float8e4
I32, I8, U8 = mybir.dt.int32, mybir.dt.int8, mybir.dt.uint8
ALU, ACT, AX = mybir.AluOpType, mybir.ActivationFunctionType, mybir.AxisListType
RMAX = bass.bass_isa.ReduceOp.max

ONE_F8 = 0x38
SLOPE = 0.2
EPS = 1e-5
VSCALE = 512.0
LEAST = 2.0 ** -22
SEG_DVE = 2
LO = 2048.0
IBT = 8
SEG = 8
RING = 4
PAIR = 2


def bass_gat(nc, x, adj, W, a1, a2, out):
    N, K = x.shape
    NH, _, D = W.shape
    NT = N // P
    KC = K // P
    IB = IBT * P
    NB = N // IB
    NG = NH // 2
    NPAIR = NT // PAIR
    NSEG = NT // SEG
    PPS = SEG // PAIR
    D1 = D + 1
    REG = 2 * D1
    PER_BANK = 512 // REG
    NACC = 2 * IBT
    NBANK = -(-NACC // PER_BANK)
    XPB = NBANK

    def acc_of(sg, t):
        return sg * IBT + t

    assert NBANK + 2 <= 8 and PPS == RING and NT % SEG == 0 and N % IB == 0

    adjt_d = nc.dram_tensor("adjt_scratch", [NB * NT // PAIR, P, PAIR, IB], U8, kind="Internal").ap()
    h_d = nc.dram_tensor("h_scratch", [N, NH * D], F32, kind="Internal").ap()
    s1_d = nc.dram_tensor("negs1_scratch", [NH * NT, P], F32, kind="Internal").ap()
    att_d = nc.dram_tensor("att_scratch", [N, NH * D1], F32, kind="Internal").ap()

    ctx = ExitStack()
    with ctx:
        def sb(name, shape, dt):
            return ctx.enter_context(nc.sbuf_tensor(name, shape, dt))

        def sem(name):
            return ctx.enter_context(nc.semaphore(name))

        ps = ctx.enter_context(nc.psum_tensor("ps", [P, 8, 512], F32))

        ADJB = NT * IB
        VB = 2 * NT * 2 * REG * 2
        big = sb("big", [P, ADJB + VB], U8)
        adjt = big[:, 0:ADJB].rearrange("p (c i) -> p c i", c=NT)
        V = big[:, ADJB:ADJB + VB].bitcast(F16).rearrange("p (h c s r) -> p h c s r", h=2, c=NT, s=2)
        y_all = big[:, 0:NT * K * 4].bitcast(F32).rearrange("p (t f) -> p t f", t=NT)

        adj_in = sb("adj_in", [P, 2, IBT, PAIR * P], I32)
        adj_bf = sb("adj_bf", [P, 2, IBT, PAIR * P], BF16)
        adj_u8 = sb("adj_u8", [P, 4, IB], U8)
        s1b = sb("s1b", [P, 2, IB], F32)
        cmp = sb("cmp", [P, RING, PAIR * IB], I8)
        pos = sb("pos", [P, RING, PAIR * IB], U8)
        neg = sb("neg", [P, RING, PAIR * IB], U8)
        raw = sb("raw", [P, NACC * REG], F32)
        comb = sb("comb", [P, NACC * D1], F32)
        num = sb("num", [P, IBT * D1], F32)
        hseg = sb("hseg", [P, 2, SEG, D1], F32)
        vtmp = sb("vtmp", [P, 2, SEG * D1], F32)
        ltmp = sb("ltmp", [P, 2, SEG * D1], F32)
        sc = sb("sc", [P, 2 * NH, NT], F32)
        negs = sb("negs", [P, 2 * NH, NT], F32)
        bd = sb("bd", [P, 2, NH, NT], F32)
        ac = sb("ac", [P, NH, 2, NT], F32)
        t1 = sb("t1", [P, NH, NT], F32)
        t2 = sb("t2", [P, NH, NT], F32)
        t3 = sb("t3", [P, NH, NT], F32)
        u = sb("u", [P, NH, NT], F32)
        cmax = sb("cmax", [P, NH], F32)
        call = sb("call", [P, NH], F32)
        hmax = sb("hmax", [P, NT], F32)
        hm = sb("hm", [P, 2], F32)
        mv2 = sb("mv2", [P, 2, 2], F32)
        okt = sb("okt", [P, NT, NH], F32)
        id32 = sb("id32", [P, P], F32)
        id16 = sb("id16", [P, P], BF16)
        zero16 = sb("zero16", [P, P], F16)
        s1r = sb("s1r", [P, NH * NT], F32)
        stats = sb("stats", [P, 2, 6], F32)
        mv = sb("mv", [P, NT, 2], F32)
        rstd = sb("rstd", [P, NT], F32)
        epsc = sb("epsc", [P, 1], F32)
        rstd2 = sb("rstd2", [P, NT], F32)
        frec = sb("frec", [P, 4, NH], F32)
        xs = cmp[:, :, :].rearrange("p a b -> p (a b)").bitcast(F32).rearrange("p (a f) -> p a f", f=K)
        hsb = pos[:, :, :].rearrange("p a b -> p (a b)").bitcast(F32).rearrange("p (a f) -> p a f", f=K)
        xT = neg[:, :, :].rearrange("p a b -> p (a b)").bitcast(F32).rearrange("p (a f) -> p a f", f=K)
        junk = big[:, ADJB + 24 * 1024:ADJB + 26 * 1024 + 0].bitcast(F32)
        hsegd = raw[:, 0:2 * SEG * D1].rearrange("p (a c f) -> p a c f", a=2, c=SEG)
        vtmpd = raw[:, 2 * SEG * D1:3 * SEG * D1]
        ltmpd = raw[:, 3 * SEG * D1:4 * SEG * D1]
        fin = adj_in[:, :, :, :].rearrange("p a t j -> p (a t j)").bitcast(F32)
        fatt = fin[:, 0:4 * NH * D1].rearrange("p (a h f) -> p a h f", a=4, h=NH)

        def f32_ring(t, pattern):
            return t.rearrange(pattern).bitcast(F32).rearrange("p (a f) -> p a f", f=K)
        fv, fr, fw = (f32_ring(m[:, :, :], "p a b -> p (a b)") for m in (cmp, pos, neg))
        fn = f32_ring(adj_bf[:, :, :, :], "p a t j -> p (a t j)")
        Wsb = big[:, ADJB:ADJB + KC * K * 4].bitcast(F32).rearrange("p (c n) -> p c n", c=KC)
        o_w = ADJB + KC * K * 4
        Wa = big[:, o_w:o_w + KC * 2 * NH * 4].bitcast(F32).rearrange("p (c n) -> p c n", c=KC)
        o_w += KC * 2 * NH * 4
        av = big[:, o_w:o_w + 2 * K * 4].bitcast(F32).rearrange("p (s n) -> p s n", s=2)
        o_w += 2 * K * 4
        wprod = big[:, o_w:o_w + 2 * KC * K * 4].bitcast(F32).rearrange("p (s c n) -> p s c n", s=2, c=KC)

        w_loaded = sem("w_loaded")
        ident_made = sem("ident_made")
        wa_step = sem("wa_step")
        x_loaded = [sem("x_loaded0"), sem("x_loaded1")]
        x_turned = sem("x_turned")
        xt_ready = sem("xt_ready")
        h_ready = sem("h_ready")
        h_copied = sem("h_copied")
        h_stored = [sem("h_stored0"), sem("h_stored1")]
        h_maxed = sem("h_maxed")
        h_sq = sem("h_sq")
        f_aggr = sem("f_aggr")
        c_part = sem("c_part")
        c_all = sem("c_all")
        tab_dve = sem("tab_dve")
        tab_act = sem("tab_act")
        s1_turned = sem("s1_turned")
        s1_stored = sem("s1_stored")
        adj_loaded = [sem("adj_loaded0"), sem("adj_loaded1")]
        adj_cast = sem("adj_cast")
        adj_turned = sem("adj_turned")
        adj_evac = sem("adj_evac")
        adj_stored = [sem("adj_stored0"), sem("adj_stored1")]
        adjt_loaded = sem("adjt_loaded")
        s1b_loaded = [sem("s1b_loaded0"), sem("s1b_loaded1")]
        cmp_act = sem("cmp_act")
        cmp_dve = sem("cmp_dve")
        pos_done = sem("pos_done")
        neg_done = sem("neg_done")
        pair_used = sem("pair_used")
        evac_act = sem("evac_act")
        evac_dve = sem("evac_dve")
        comb_step = sem("comb_step")
        raw_used = sem("raw_used")
        att_stored = sem("att_stored")
        hd_loaded = [sem("hd_loaded0"), sem("hd_loaded1")]
        hp_loaded = [sem("hp_loaded0"), sem("hp_loaded1")]
        vstep_dve = sem("vstep_dve")
        vstep_pool = sem("vstep_pool")
        v_built = [sem("v_built0"), sem("v_built1")]
        v_first = sem("v_first")
        fatt_loaded = [sem(f"fatt_loaded{q}") for q in range(4)]
        fx_loaded = [sem(f"fx_loaded{q}") for q in range(4)]
        f_rec = sem("f_rec")
        f_ok = sem("f_ok")
        f_val = sem("f_val")
        f_relu = sem("f_relu")
        f_exp = sem("f_exp")
        f_elu = sem("f_elu")
        f_sum = sem("f_sum")
        f_bn = sem("f_bn")
        f_var = sem("f_var")
        f_std = sem("f_std")
        f_rstd = sem("f_rstd")
        f_out = sem("f_out")
        out_stored = sem("out_stored")

        passed_pe, passed_dve, passed_pool, passed_sp = (
            sem(f"passed_{e}") for e in ("pe", "dve", "pool", "sp"))

        C_TURNED, C_HREADY, C_HCOP, C_MAX, C_CAST, C_CHUNK, C_EV = 2, 2, 2, 2, 2, 3, 2
        C_RING, C_BANK, C_FIN = RING, NBANK // 2, 4
        C_CMP, C_NEG, C_DMA = 1, 1, 16

        adj_r = adj.rearrange("(b t p) j -> b p t j", t=IBT, p=P)
        x_r = x.rearrange("(t p) f -> t p f", p=P)
        out_r = out.rearrange("(t p) f -> t p f", p=P)
        att_r = att_d.rearrange("(t p) (h f) -> t p h f", p=P, h=NH)
        att_b = att_d.rearrange("(b t p) (h f) -> b h p t f", t=IBT, p=P, h=NH)
        h_r = h_d.rearrange("(t p) f -> t p f", p=P)
        h_s = h_d.rearrange("(s c p) (h f) -> s h p c f", c=SEG, p=P, h=NH)
        s1_rows = s1_d.rearrange("(h b t) p -> (h b) (t p)", h=NH, t=IBT)
        adjt_s = adjt_d.rearrange("(s m) p a i -> s p m (a i)", m=PPS)
        adjt32 = big[:, 0:ADJB].bitcast(I32)
        pos32, neg32, cmp32 = (a[:, :, :].bitcast(I32) for a in (pos, neg, cmp))
        pos8, neg8 = pos[:, :, :].bitcast(F8), neg[:, :, :].bitcast(F8)
        W32 = PAIR * IB // 4
        ACT_ONLY = {False: (0, 2), True: (0,)}
        DVE_CMP = {k: PPS - len(v) for k, v in ACT_ONLY.items()}

        block = ctx.enter_context(nc.Block())

        @block.sync
        def _(sp):
            def load_unit(b, k, i):
                sp.wait_ge(adj_cast, b * NPAIR + k + 1 - 2 + C_CAST)
                sp.dma_start(adj_in[:, i], adj_r[b, :, :, bass.ds(k * (PAIR * P), PAIR * P)]
                             ).then_inc(adj_loaded[i], 16)

            def load_adjt(n, b, s, used):
                sp.wait_ge(neg_done, used + C_NEG)
                for e in range(2):
                    sp.wait_ge(adj_stored[e], (b * (NPAIR // 2) + (s + 1) * (PPS // 2)) * 16 + C_DMA)
                sp.wait_ge(adjt_loaded, n * 16)
                sp.sem_inc(passed_sp, 1)
                sp.dma_start(adjt[:, s * SEG:(s + 1) * SEG, :].rearrange("p (m a) i -> p m (a i)", a=PAIR),
                             adjt_s[b * NSEG + s]).then_inc(adjt_loaded, 16)

            def load_s1(head, b, hd, used):
                sp.wait_ge(cmp_act, used + C_CMP)
                sp.sem_inc(passed_sp, 1)
                sp.wait_ge(pos_done, used + C_RING)
                sp.sem_inc(passed_sp, 1)
                sp.dma_start(s1b[:, hd], s1_rows[head * NB + b].partition_broadcast(P)
                             ).then_inc(s1b_loaded[hd], 16)

            for c in range(KC):
                sp.dma_start(Wsb[:, c].rearrange("p (h f) -> p h f", h=NH),
                             W[:, c * P:(c + 1) * P, :].rearrange("h p f -> p h f")).then_inc(w_loaded, 16)
            for s, a in enumerate((a1, a2)):
                sp.dma_start(av[:, s], a.rearrange("h f -> (h f)").partition_broadcast(P)).then_inc(w_loaded, 16)

            with sp.Fori(0, NT // 4) as i:
                for j in range(4):
                    sp.wait_ge(x_turned, i * 4 + j + 1 - 2 + C_TURNED)
                    sp.dma_start(xs[:, j % 2], x_r[i * 4 + j]).then_inc(x_loaded[j % 2], 16)
                    if j % 2:
                        load_unit(0, i * 2 + j // 2, j // 2)

            for e in range(2):
                sp.wait_ge(h_stored[e], NT // 2 * 16 + C_DMA)
            sp.wait_ge(ident_made, 1)
            for s in range(SEG_DVE):
                sp.dma_start(hsegd[:, s, :, 0:D], h_s[s, 0]).then_inc(hd_loaded[s], 16)
            sp.wait_ge(s1_stored, 16)
            load_s1(0, 0, 0, 0)
            for s in range(NSEG - 2):
                load_adjt(s, 0, s, 0)

            def iteration(g, b, nxt, T, produce):
                for s in range(NSEG):
                    if produce:
                        for i in range(2):
                            load_unit(b + 1, 2 * s + i, i)
                    if s == 1:
                        load_s1(g * 2 + 1, b, 1, T * (2 * NPAIR))
                    if s < 2:
                        load_adjt(T * NSEG + NSEG - 2 + s, b, NSEG - 2 + s, T * (2 * NPAIR))
                for s in range(NSEG):
                    if produce:
                        for i in range(2):
                            load_unit(b + 1, NPAIR // 2 + 2 * s + i, i)
                    if nxt and s == 1:
                        load_s1(nxt[0] * 2, nxt[1], 0, T * (2 * NPAIR) + NPAIR)
                    if nxt and s >= 2:
                        load_adjt((T + 1) * NSEG + s - 2, nxt[1], s - 2,
                                  T * (2 * NPAIR) + NPAIR + PPS * (s - 1))

            with sp.Fori(0, NB - 1) as b:
                iteration(0, b, (0, b + 1), b, True)
            iteration(0, NB - 1, (1, 0), NB - 1, False)
            with sp.Fori(1, NG - 1) as g:
                with sp.Fori(0, NB - 1) as b:
                    iteration(g, b, (g, b + 1), g * NB + b, False)
                iteration(g, NB - 1, (g + 1, 0), g * NB + NB - 1, False)
            with sp.Fori(0, NB - 1) as b:
                iteration(NG - 1, b, (NG - 1, b + 1), (NG - 1) * NB + b, False)
            iteration(NG - 1, NB - 1, None, NG * NB - 1, False)

            sp.wait_ge(att_stored, 16 * 2 * NG * NB)
            sp.wait_ge(pair_used, 2 * NG * NB * NPAIR + C_RING)
            sp.wait_ge(neg_done, 2 * NG * NB * NPAIR + C_NEG)
            with sp.Fori(0, NT // 4) as i:
                for q in range(4):
                    t = i * 4 + q
                    sp.wait_ge(f_val, t + 1 - 4 + C_FIN)
                    sp.wait_ge(f_ok, t + 1 - 4 + C_FIN)
                    sp.wait_ge(f_sum, t + 1 - 4 + C_FIN)
                    sp.dma_start(fatt[:, q], att_r[t]).then_inc(fatt_loaded[q], 16)
                    sp.dma_start(y_all[:, t, :], x_r[t]).then_inc(fx_loaded[q], 16)
            with sp.Fori(0, NT) as t:
                sp.wait_ge(f_out, t + 1)
                sp.dma_start(out_r[t], y_all[:, t, :]).then_inc(out_stored, 16)
            sp.wait_ge(out_stored, 16 * NT)

        @block.scalar
        def _(act):
            def evac_chunk(c4, q):
                act.wait_ge(adj_turned, c4 * 4 + q + 1 + C_CHUNK)
                if q % 2 == 0:
                    act.wait_ge(adj_stored[q // 2], c4 * 16 + C_DMA)
                act.copy(adj_u8[:, q], ps[:, XPB + q % 2].bitcast(BF16)).then_inc(adj_evac, 1)
                if q % 2:
                    act.wait_ge(adj_evac, c4 * 4 + q + 1 + C_EV)
                    act.dma_start(adjt_d[c4 * 2 + q // 2], adj_u8[:, q - 1:q + 1]
                                  ).then_inc(adj_stored[q // 2], 16)

            def stage1(i, evacs):
                for q in range(4):
                    t, j = i * 4 + q, q % 2
                    act.wait_ge(h_ready, t + 1 + C_HREADY)
                    act.wait_ge(h_stored[j], (i * 2 + q // 2) * 16 + C_DMA)
                    act.wait_ge(h_maxed, t + 1 - 2 + C_MAX)
                    act.copy(sc[:, :, t], ps[:, 4 + j, 0:2 * NH])
                    act.copy(hsb[:, j], ps[:, 2 + j]).then_inc(h_copied, 1)
                    act.wait_ge(h_copied, t + 1 + C_HCOP)
                    act.dma_start(h_r[t], hsb[:, j]).then_inc(h_stored[j], 16)
                    if q < evacs:
                        evac_chunk(i, q)

            with act.Fori(0, NT // 4 - 1) as i:
                stage1(i, 4)
            stage1(NT // 4 - 1, 2)

            act.wait_ge(tab_dve, 1)
            act.activation(bd[:, 0], t1[:, :, :], ACT.Exp).then_inc(tab_act, 1)
            act.activation(bd[:, 1], t1[:, :, :], ACT.Exp, scale=SLOPE).then_inc(tab_act, 1)
            act.wait_ge(tab_dve, 3)
            act.activation(ac[:, :, 0, :], t2[:, :, :], ACT.Exp).then_inc(tab_act, 1)
            act.activation(ac[:, :, 1, :], t3[:, :, :], ACT.Exp).then_inc(tab_act, 1)
            act.wait_ge(tab_dve, 4)

            def evac_banks(H):
                act.wait_ge(pair_used, (H + 1) * NPAIR + C_RING)
                act.wait_ge(raw_used, H)
                for n in range(0, NBANK, 2):
                    w = min(PER_BANK, NACC - n * PER_BANK) * REG
                    act.copy(raw[:, n * PER_BANK * REG:n * PER_BANK * REG + w], ps[:, n, 0:w]
                             ).then_inc(evac_act, 1)

            def segment(g, hd, T, s, produce, after=None):
                for q in range(PPS):
                    pair = (T * 2 + hd) * NPAIR + s * PPS + q
                    act.wait_ge(pos_done, pair + 1 - RING + C_RING)
                    for c in range(PAIR):
                        if c == 0 or q in ACT_ONLY[produce]:
                            i = act.activation(
                                cmp[:, q, c * IB:(c + 1) * IB], s1b[:, hd], ACT.Sign,
                                bias=negs[:, NH + g * 2 + hd, bass.ds(s * SEG + q * PAIR + c, 1)])
                    i.then_inc(cmp_act, 1)
                    if after:
                        after(s, q)

            def head(g, hd, T, produce, flush=False, first=False):
                act.wait_ge(s1b_loaded[hd], T * 16 + 16)
                n4 = T * (NPAIR // 2) + hd * NSEG + NT // 4 - 1

                def after(s, q):
                    evac_chunk(n4 + s + (1 + q) // 4, (1 + q) % 4)

                def after_first(s, q):
                    if (produce and not (first and q == 0)) or (flush and hd == 0 and q < 3):
                        after(s, q)
                    if q == 2 and not first:
                        evac_banks(T * 2 + hd - 1)
                segment(g, hd, T, 0, produce, after_first)
                with act.Fori(1, NSEG) as s:
                    segment(g, hd, T, s, produce, after if produce else None)

            head(0, 0, 0, True, first=True)
            head(0, 1, 0, True)
            with act.Fori(1, NB - 1) as b:
                for hd in range(2):
                    head(0, hd, b, True)
            for hd in range(2):
                head(0, hd, NB - 1, False, flush=True)
            with act.Fori(1, NG) as g:
                with act.Fori(0, NB) as b:
                    for hd in range(2):
                        head(g, hd, g * NB + b, False)
            evac_banks(2 * NG * NB - 1)

            with act.Fori(0, NT // 4) as i:
                for q in range(4):
                    t = i * 4 + q
                    act.wait_ge(f_val, t + 1 + C_FIN)
                    act.wait_ge(f_elu, t + 1 - 4 + C_FIN)
                    act.activation(fn[:, q], fv[:, q], ACT.Relu, scale=-1.0).then_inc(f_relu, 1)
                    act.activation(fr[:, q], fv[:, q], ACT.Relu)
                    act.wait_ge(f_relu, t + 1)
                    act.activation(fn[:, q], fn[:, q], ACT.Exp, scale=-1.0).then_inc(f_exp, 1)
            act.wait_ge(f_var, NT + 1)
            act.wait_ge(ident_made, 1)
            act.activation(rstd[:, :], mv[:, :, 1], ACT.Sqrt, bias=epsc[:, 0:1]).then_inc(f_std, 1)

        @block.vector
        def _(dve):
            dve.sem_inc(adj_cast, C_CAST)
            dve.sem_inc(h_maxed, C_MAX)
            dve.sem_inc(pos_done, C_RING)
            dve.sem_inc(evac_dve, C_BANK)
            dve.sem_inc(neg_done, C_NEG)
            for f in (f_val, f_ok, f_elu, f_sum):
                dve.sem_inc(f, C_FIN)
            dve.sem_inc(f_aggr, 2)
            dve.sem_inc(f_var, 1)

            dve.wait_ge(w_loaded, 16 * (KC + 2))
            for s in range(2):
                dve.tensor_tensor(wprod[:, s], Wsb, av[:, s:s + 1, :].to_broadcast([P, KC, NH * D]),
                                  ALU.mult).then_inc(wa_step, 1)
            for s in range(2):
                dve.wait_ge(wa_step, s + 1)
                dve.tensor_reduce(Wa[:, :, s * NH:(s + 1) * NH],
                                  wprod[:, s].rearrange("p c (h f) -> p c h f", h=NH), AX.X, ALU.add
                                  ).then_inc(wa_step, 1)

            def cast_unit(b, k, half, i):
                un = b * NPAIR + k
                dve.wait_ge(adj_loaded[i], half * 16 + 16)
                dve.wait_ge(adj_turned, un * 2 - 2 + C_CHUNK)
                dve.tensor_scalar(adj_bf[:, i], adj_in[:, i], 0.0, float(ONE_F8), ALU.is_gt, ALU.mult
                                  ).then_inc(adj_cast, 1)

            def largest(t, j):
                dve.wait_ge(h_copied, t + 1 + C_HCOP)
                dve.wait_ge(h_maxed, t + C_MAX)
                dve.sem_inc(passed_dve, 1)
                dve.tensor_tensor_reduce(junk, hsb[:, j], hsb[:, j], 1.0, 0.0, ALU.mult, ALU.max,
                                         hm[:, j:j + 1]).then_inc(h_sq, 1)
                dve.wait_ge(h_sq, t + 1)
                dve.tensor_copy(hmax[:, bass.ds(t, 1)], hm[:, j:j + 1]).then_inc(h_maxed, 1)

            def stage1(i, first=False):
                for q in range(0, 4, 2):
                    cast_unit(0, i * 2 + q // 2, i, q // 2)
                    for j in range(2):
                        t = i * 4 + q + j
                        dve.wait_ge(x_turned, t + 1 + C_TURNED)
                        dve.wait_ge(h_ready, t + 1 - 2 + C_HREADY)
                        dve.tensor_copy(xT[:, j], ps[:, j]).then_inc(xt_ready, 1)
                    if not (first and q == 0):
                        for j in range(2):
                            largest(i * 4 + q - 2 + j, j)

            dve.wait_ge(wa_step, 4)
            stage1(0, True)
            with dve.Fori(1, NT // 4) as i:
                stage1(i)
            for j in range(2):
                largest(NT - 2 + j, j)

            dve.wait_ge(h_copied, NT + C_HCOP)
            dve.tensor_reduce(cmax[:, :], sc[:, NH:2 * NH, :], AX.X, ALU.max).then_inc(c_part, 1)
            dve.wait_ge(c_all, 1)
            call_b = call[:, :].unsqueeze(2).to_broadcast([P, NH, NT])
            dve.tensor_tensor(t1[:, :, :], sc[:, NH:2 * NH, :], call_b, ALU.subtract).then_inc(tab_dve, 1)
            dve.tensor_tensor(u[:, :, :], sc[:, 0:NH, :], call_b, ALU.add).then_inc(vstep_dve, 1)
            dve.wait_ge(vstep_dve, 1)
            dve.tensor_scalar(t2[:, :, :], u[:, :, :], 1.0 - SLOPE, 0.0, ALU.mult, ALU.min).then_inc(tab_dve, 1)
            dve.tensor_scalar(t3[:, :, :], u[:, :, :], SLOPE - 1.0, 0.0, ALU.mult, ALU.min).then_inc(tab_dve, 1)
            dve.tensor_scalar(negs[:, :, :], sc[:, :, :], -1.0, None, ALU.mult).then_inc(tab_dve, 1)
            dve.wait_ge(tab_act, 2)
            dve.tensor_scalar(bd[:, :, :, :], bd[:, :, :, :], VSCALE, None, ALU.mult).then_inc(tab_dve, 1)
            dve.wait_ge(s1_turned, 1)
            dve.tensor_copy(s1r[:, :], ps[:, 0, 0:NH * NT]).then_inc(tab_dve, 1)

            def build(eng, step, base, hseg_, v_, l_, hd, s, head, done):
                for sg in range(2):
                    k = base + sg * 4
                    fac = bd[:, sg, head, s * SEG:(s + 1) * SEG].unsqueeze(2).to_broadcast([P, SEG, D1])
                    v3, l3 = (a.rearrange("p (c f) -> p c f", c=SEG) for a in (v_, l_))
                    dst = V[:, hd, s * SEG:(s + 1) * SEG, sg]
                    eng.wait_ge(step, k)
                    eng.tensor_tensor(v3, hseg_, fac, ALU.mult).then_inc(step, 1)
                    eng.wait_ge(step, k + 1)
                    eng.tensor_copy(dst[:, :, 0:D1], v3).then_inc(step, 1)
                    eng.wait_ge(step, k + 2)
                    eng.tensor_tensor(l3, v3, dst[:, :, 0:D1], ALU.subtract).then_inc(step, 1)
                    eng.wait_ge(step, k + 3)
                    i = eng.tensor_scalar(dst[:, :, D1:REG], l3, LO, None, ALU.mult)
                    i.then_inc(step, 1)
                eng.wait_ge(step, base + 8)
                eng.sem_inc(done, 1)

            dve.wait_ge(tab_dve, 5)
            dve.wait_ge(h_maxed, NT + C_MAX)
            dve.wait_ge(h_ready, NT + C_HREADY)
            for s in range(SEG_DVE):
                dve.wait_ge(hd_loaded[s], 16)
                build(dve, vstep_dve, 8 * s + 1, hsegd[:, s], vtmpd, ltmpd, 0, s, 0, v_first)

            def evac_bank(n, H):
                dve.wait_ge(raw_used, H)
                w = min(PER_BANK, NACC - n * PER_BANK) * REG
                dve.tensor_copy(raw[:, n * PER_BANK * REG:n * PER_BANK * REG + w], ps[:, n, 0:w]
                                ).then_inc(evac_dve, 1)

            def evac_banks(H):
                dve.wait_ge(pair_used, (H + 1) * NPAIR + C_RING)
                for n in range(1, NBANK, 2):
                    evac_bank(n, H)

            def segment(g, hd, T, s, produce, b=None, evac=None):
                base = (T * 2 + hd) * NPAIR + s * PPS
                n = 0
                for q in range(PPS):
                    pair = base + q
                    if evac is not None and q == PPS - 1:
                        evac_banks(evac)
                    if q not in ACT_ONLY[produce]:
                        dve.wait_ge(pos_done, pair + 1 - RING + C_RING)
                        dve.tensor_scalar(cmp[:, q, IB:2 * IB], s1b[:, hd],
                                          sc[:, NH + g * 2 + hd, bass.ds(s * SEG + q * PAIR + 1, 1)],
                                          -1.0, ALU.is_lt, ALU.mult).then_inc(cmp_dve, 1)
                        n += 1
                        n4 = (T * 2 + hd) * NSEG + s
                        past = 0 if produce else (NB - 1) * 2 * NSEG * (DVE_CMP[True] - DVE_CMP[False])
                        dve.wait_ge(cmp_dve, n4 * DVE_CMP[produce] + past + n)
                    dve.wait_ge(cmp_act, pair + 1 + C_CMP)
                    dve.wait_ge(pair_used, pair + 1 - RING + C_RING)
                    a = adjt32[:, bass.ds((s * PPS + q) * W32, W32)]
                    dve.tensor_tensor(pos32[:, q], cmp32[:, q], a, ALU.bitwise_and).then_inc(pos_done, 1)
                    dve.wait_ge(pos_done, pair + 1 + C_RING)
                    dve.tensor_tensor(neg32[:, q], pos32[:, q], a, ALU.bitwise_xor).then_inc(neg_done, 1)
                    if produce and q % 2:
                        cast_unit(b + 1, hd * (NPAIR // 2) + s * 2 + q // 2,
                                  (b + 1) * (NPAIR // 2) + hd * (NPAIR // 4) + s, q // 2)

            def head(g, hd, T, produce, b=None, first=False):
                dve.wait_ge(s1b_loaded[hd], T * 16 + 16)
                if hd == 0:
                    dve.wait_ge(adjt_loaded, T * (16 * NSEG) + 16)
                segment(g, hd, T, 0, produce, b, None if first else T * 2 + hd - 1)
                with dve.Fori(1, NSEG) as s:
                    if hd == 0:
                        dve.wait_ge(adjt_loaded, (T * NSEG + s) * 16 + 16)
                    segment(g, hd, T, s, produce, b)

            head(0, 0, 0, True, 0, first=True)
            head(0, 1, 0, True, 0)
            with dve.Fori(1, NB - 1) as b:
                for hd in range(2):
                    head(0, hd, b, True, b)
            for hd in range(2):
                head(0, hd, NB - 1, False)
            with dve.Fori(1, NG) as g:
                with dve.Fori(0, NB) as b:
                    for hd in range(2):
                        head(g, hd, g * NB + b, False)
            evac_banks(2 * NG * NB - 1)

            def invert(t, q, n16):
                dve.wait_ge(fatt_loaded[q], n16 * 16 + 16)
                dve.wait_ge(f_val, t + 1 - 4 + C_FIN)
                dve.reciprocal(frec[:, q], fatt[:, q, :, D]).then_inc(f_rec, 1)
                dve.tensor_scalar(okt[:, bass.ds(t, 1), :].rearrange("p a h -> p (a h)"), fatt[:, q, :, D],
                                  VSCALE * LEAST, None, ALU.is_ge).then_inc(f_ok, 1)

            def elu(t, q):
                dve.wait_ge(f_exp, t + 1)
                dve.wait_ge(f_sum, t + 1 - 4 + C_FIN)
                dve.scalar_tensor_tensor(fw[:, q], fn[:, q], -1.0, fr[:, q], ALU.add, ALU.add
                                         ).then_inc(f_elu, 1)

            def statistics(t, q):
                j = q % 2
                dve.wait_ge(f_sum, t + 1 + C_FIN)
                dve.wait_ge(f_aggr, t + 1 - 2 + 2)
                dve.bn_stats(stats[:, j], y_all[:, t, :]).then_inc(f_bn, 1)
                dve.wait_ge(f_bn, t + 1)
                dve.wait_ge(f_var, t + 1)
                dve.sem_inc(passed_dve, 1)
                dve.bn_aggr(mv2[:, j], stats[:, j]).then_inc(f_aggr, 1)
                dve.wait_ge(f_aggr, t + 1 + 2)
                dve.tensor_copy(mv[:, t, :], mv2[:, j]).then_inc(f_var, 1)

            def last_stage(i, first=False):
                for q in range(4):
                    t = i * 4 + q
                    invert(t, q, i)
                    if not first or q >= 2:
                        elu(t - 2, (q - 2) % 4)
                    if not first:
                        statistics(t - 4, q)

            last_stage(0, True)
            with dve.Fori(1, NT // 4) as i:
                last_stage(i)
            for t in (NT - 2, NT - 1):
                elu(t, t % 4)
            for t in range(NT - 4, NT):
                statistics(t, t % 4)
            dve.wait_ge(f_std, 1)
            dve.reciprocal(rstd2[:, :], rstd[:, :]).then_inc(f_rstd, 1)
            dve.wait_ge(f_rstd, 1)
            with dve.Fori(0, NT) as t:
                dve.tensor_scalar(y_all[:, t, :], y_all[:, t, :], mv[:, t, 0:1], rstd2[:, bass.ds(t, 1)],
                                  ALU.subtract, ALU.mult).then_inc(f_out, 1)

        @block.tensor
        def _(pe):
            pe.sem_inc(x_turned, C_TURNED)
            pe.sem_inc(h_ready, C_HREADY)
            pe.sem_inc(adj_turned, C_CHUNK)
            pe.sem_inc(pair_used, C_RING)
            pe.wait_ge(ident_made, 1)

            def turn_adj(u, chunk, q):
                pe.wait_ge(adj_cast, u + 1 + C_CAST)
                pe.wait_ge(adj_evac, chunk + 1 - 2 + C_EV)
                pst = ps[:, XPB + q % 2].bitcast(BF16)
                for t in range(IBT):
                    i = pe.transpose(pst[:, t * P:(t + 1) * P],
                                     adj_bf[:, q // 2, t, q % 2 * P:(q % 2 + 1) * P], id16[:, :])
                i.then_inc(adj_turned, 1)

            def tile_h(t, j):
                pe.wait_ge(xt_ready, t + 1)
                pe.wait_ge(h_copied, t + 1 - 2 + C_HCOP)
                for c in range(KC):
                    pe.matmul(ps[:, 2 + j], xT[:, j, c * P:(c + 1) * P], Wsb[:, c], start=(c == 0),
                              stop=(c == KC - 1))
                for c in range(KC):
                    i = pe.matmul(ps[:, 4 + j, 0:2 * NH], xT[:, j, c * P:(c + 1) * P], Wa[:, c],
                                  start=(c == 0), stop=(c == KC - 1))
                i.then_inc(h_ready, 1)

            pe.wait_ge(wa_step, 4)
            with pe.Fori(0, NT // 4) as i:
                for q in range(0, 4, 2):
                    for j in range(2):
                        t = i * 4 + q + j
                        pe.wait_ge(x_loaded[j], (i * 2 + q // 2) * 16 + 16)
                        pe.wait_ge(h_ready, t + 1 - 2 + C_HREADY)
                        for c in range(KC):
                            n = pe.transpose(ps[:, j, c * P:(c + 1) * P], xs[:, j, c * P:(c + 1) * P], id32[:, :])
                        n.then_inc(x_turned, 1)
                    for j in range(2):
                        turn_adj(i * 2 + q // 2, i * 4 + q + j, q + j)
                    for j in range(2):
                        tile_h(i * 4 + q + j, j)

            pe.wait_ge(tab_dve, 4)
            pe.wait_ge(xt_ready, NT)
            n1 = negs[:, 0:NH, :].rearrange("p h t -> p (h t)")
            for c in range(NH * NT // P):
                i = pe.transpose(ps[:, 0, c * P:(c + 1) * P], n1[:, c * P:(c + 1) * P], id32[:, :])
            i.then_inc(s1_turned, 1)
            pe.wait_ge(tab_dve, 6)
            pe.wait_ge(h_copied, NT + C_HCOP)

            def block_sums(g, T, produce, b=None):
                for hd in range(2):
                    H = T * 2 + hd
                    for k in range(NPAIR):
                        q = k % RING
                        if hd == 0 and k % PPS == 0 and k // PPS < SEG_DVE:
                            pe.wait_ge(v_first, k // PPS + 1)
                        if k % PPS == 0:
                            pe.wait_ge(v_built[hd], g * NSEG + k // PPS + 1)
                        for c in range(PAIR):
                            for sg, masks, done, credit in ((0, pos8, pos_done, C_RING), (1, neg8, neg_done, C_NEG)):
                                if c == 0:
                                    pe.wait_ge(done, H * NPAIR + k + 1 + credit)
                                    pe.sem_inc(passed_pe, 1)
                                for t in range(IBT):
                                    r = acc_of(sg, t)
                                    bank, off = r // PER_BANK, r % PER_BANK * REG
                                    if k == 0 and c == 0 and r % PER_BANK == 0:
                                        ev = evac_dve if bank % 2 else evac_act
                                        pe.wait_ge(ev, H * C_BANK - C_BANK + bank // 2 + 1 + C_BANK)
                                        pe.matmul(ps[:, bank, 0:2], zero16[:, :], zero16[:, 0:2], start=True,
                                                  stop=False, skip_group_check=True)
                                    i = pe.matmul(ps[:, bank, off:off + REG],
                                                  masks[:, q, c * IB + t * P:c * IB + (t + 1) * P],
                                                  V[:, hd, k * PAIR + c, sg, :], start=False,
                                                  stop=(k == NPAIR - 1 and c == PAIR - 1),
                                                  skip_group_check=True)
                        i.then_inc(pair_used, 1)
                        if produce:
                            turn_adj((b + 1) * NPAIR + hd * (NPAIR // 2) + k // 2,
                                     (b + 1) * NT + hd * NPAIR + k, k % 4)

            with pe.Fori(0, NB - 1) as b:
                block_sums(0, b, True, b)
            block_sums(0, NB - 1, False)
            with pe.Fori(1, NG) as g:
                with pe.Fori(0, NB) as b:
                    block_sums(g, g * NB + b, False)

        @block.gpsimd
        def _(pool):
            pool.sem_inc(h_copied, C_HCOP)
            pool.sem_inc(adj_evac, C_EV)
            pool.sem_inc(evac_act, C_BANK)
            pool.sem_inc(cmp_act, C_CMP)
            for d in (*h_stored, *adj_stored):
                pool.sem_inc(d, C_DMA)
            for m in (id32, id16):
                pool.memset(m[:, :], 0.0).then_inc(comb_step, 1)
            pool.wait_ge(comb_step, 2)
            for m in (id32, id16):
                pool.affine_select(out=m[:, :], in_=m[:, :], compare_op=ALU.not_equal, fill=1.0, base=0,
                                   pattern=[[-1, P]], channel_multiplier=1).then_inc(comb_step, 1)
            pool.memset(zero16[:, :], 0.0).then_inc(comb_step, 1)
            pool.memset(epsc[:, :], EPS).then_inc(comb_step, 1)
            pool.memset(hseg[:, :, :, D:D1], 1.0).then_inc(comb_step, 1)
            pool.memset(hsegd[:, :, :, D:D1], 1.0).then_inc(comb_step, 1)
            pool.sem_inc(vstep_pool, 1)
            pool.sem_inc(v_built[0], SEG_DVE)
            pool.wait_ge(comb_step, 8)
            pool.sem_inc(ident_made, 1)

            pool.wait_ge(c_part, 1)
            pool.partition_all_reduce(call[:, :], cmax[:, :], P, RMAX).then_inc(c_all, 1)
            pool.wait_ge(tab_dve, 6)
            pool.dma_start(s1_d.rearrange("(q r) p -> r q p", r=P),
                           s1r[:, :].rearrange("p (q r) -> p q r", r=P)).then_inc(s1_stored, 16)

            def load_h(m, i, head, s):
                pool.wait_ge(vstep_pool, 8 * (m - 1) + 1)
                pool.dma_start(hseg[:, i, :, 0:D], h_s[s, head]).then_inc(hp_loaded[i], 16)

            def build_segment(m, hm_, i, hd, head, s):
                pool.wait_ge(hp_loaded[i], hm_ * 16 + 16)
                for sg in range(2):
                    k = m * 8 + sg * 4 + 1
                    fac = bd[:, sg, head, s * SEG:(s + 1) * SEG].unsqueeze(2).to_broadcast([P, SEG, D1])
                    v3 = vtmp[:, sg].rearrange("p (c f) -> p c f", c=SEG)
                    l3 = ltmp[:, sg].rearrange("p (c f) -> p c f", c=SEG)
                    dst = V[:, hd, s * SEG:(s + 1) * SEG, sg]
                    pool.wait_ge(vstep_pool, k)
                    pool.tensor_tensor(v3, hseg[:, i], fac, ALU.mult).then_inc(vstep_pool, 1)
                    pool.wait_ge(vstep_pool, k + 1)
                    pool.sem_inc(passed_pool, 1)
                    pool.tensor_scalar(dst[:, :, 0:D1], v3, 1.0, 1.0, ALU.mult, ALU.mult).then_inc(vstep_pool, 1)
                    pool.wait_ge(vstep_pool, k + 2)
                    pool.tensor_tensor(l3, v3, dst[:, :, 0:D1], ALU.subtract).then_inc(vstep_pool, 1)
                    pool.wait_ge(vstep_pool, k + 3)
                    pool.sem_inc(passed_pool, 1)
                    pool.tensor_scalar(dst[:, :, D1:REG], l3, LO, 1.0, ALU.mult, ALU.mult
                                       ).then_inc(vstep_pool, 1)
                pool.wait_ge(vstep_pool, m * 8 + 8 + 1)
                pool.sem_inc(v_built[hd], 1)

            def build_first():
                todo = [(0, s) for s in range(SEG_DVE, NSEG)] + [(1, s) for s in range(NSEG)]
                for m in range(2):
                    pool.dma_start(hseg[:, m, :, 0:D], h_s[todo[m][1], todo[m][0]]).then_inc(hp_loaded[m], 16)
                for m, (hd, s) in enumerate(todo):
                    build_segment(m, m // 2, m % 2, hd, hd, s)
                    if m + 2 < len(todo):
                        load_h(m + 2, m % 2, todo[m + 2][0], todo[m + 2][1])
                return len(todo)

            def combine(g, hd, b, T):
                H = T * 2 + hd
                head = g * 2 + hd
                st = 8 + H * 4
                pool.wait_ge(evac_act, H * C_BANK + C_BANK + C_BANK)
                pool.wait_ge(evac_dve, H * C_BANK + C_BANK + C_BANK)
                r3 = raw[:, :].rearrange("p (r f) -> p r f", r=NACC)
                c3 = comb[:, :].rearrange("p (r f) -> p r f", r=NACC)
                pool.wait_ge(comb_step, st)
                pool.sem_inc(passed_pool, 1)
                pool.tensor_scalar(c3, r3[:, :, D1:REG], 1.0 / LO, 1.0, ALU.mult, ALU.mult).then_inc(comb_step, 1)
                pool.wait_ge(comb_step, st + 1)
                pool.tensor_tensor(c3, c3, r3[:, :, 0:D1], ALU.add).then_inc(comb_step, 1)
                pool.wait_ge(comb_step, st + 2)
                pool.sem_inc(raw_used, 1)
                fac = ac[:, head, :, bass.ds(b * IBT, IBT)].unsqueeze(3).to_broadcast([P, 2, IBT, D1])
                c4 = comb[:, :].rearrange("p (s t f) -> p s t f", s=2, f=D1)
                pool.tensor_tensor(c4, c4, fac, ALU.mult).then_inc(comb_step, 1)
                pool.wait_ge(comb_step, st + 3)
                pool.tensor_tensor(num[:, :].rearrange("p (t f) -> p t f", t=IBT), c4[:, 0], c4[:, 1],
                                   ALU.add).then_inc(comb_step, 1)
                pool.wait_ge(comb_step, st + 4)
                pool.dma_start(att_b[b, head], num[:, :].rearrange("p (t f) -> p t f", t=IBT)
                               ).then_inc(att_stored, 16)
                pool.wait_ge(att_stored, H * 16 + 16)

            pool.wait_ge(tab_dve, 5)
            for e in range(2):
                pool.wait_ge(h_stored[e], NT // 2 * 16 + C_DMA)
            pool.wait_ge(h_ready, NT + C_HREADY)
            pool.wait_ge(h_maxed, NT + C_MAX)
            NFIRST = build_first()
            pool.wait_ge(tab_act, 4)

            def build_next(g, hd, T):
                m0 = (g * 2 + hd) * NSEG + NFIRST
                for s in range(2):
                    load_h(m0 + s, s, g * 2 + 2 + hd, s)
                for s in range(NSEG):
                    pool.wait_ge(pair_used, (T * 2 + hd) * NPAIR + PPS * (s + 1) + C_RING)
                    build_segment(m0 + s, (g * 2 + hd) * (NSEG // 2) + NFIRST // 2 + s // 2, s % 2, hd,
                                  g * 2 + 2 + hd, s)
                    if s + 2 < NSEG:
                        load_h(m0 + s + 2, s % 2, g * 2 + 2 + hd, s + 2)

            def group(g):
                with pool.Fori(0, NB - 1) as b:
                    for hd in range(2):
                        combine(g, hd, b, g * NB + b)
                T = g * NB + NB - 1
                for hd in range(2):
                    build_next(g, hd, T)
                    combine(g, hd, NB - 1, T)

            with pool.Fori(0, NG - 1) as g:
                group(g)
            with pool.Fori(0, NB) as b:
                for hd in range(2):
                    combine(NG - 1, hd, b, (NG - 1) * NB + b)

            pool.wait_ge(neg_done, 2 * NG * NB * NPAIR + C_NEG)
            pool.wait_ge(pair_used, 2 * NG * NB * NPAIR + C_RING)

            first_four = None

            def values(t, q, n16):
                pool.wait_ge(f_rec, t + 1)
                if n16 is not first_four:
                    pool.wait_ge(f_exp, t + 1 - 4)
                pool.tensor_tensor(fv[:, q].rearrange("p (h f) -> p h f", h=NH), fatt[:, q, :, 0:D],
                                   frec[:, q].unsqueeze(2).to_broadcast([P, NH, D]), ALU.mult
                                   ).then_inc(f_val, 1)

            def residual(t, q, n16):
                pool.wait_ge(f_elu, t + 1 + C_FIN)
                pool.wait_ge(fx_loaded[q], n16 * 16 + 16)
                pool.tensor_tensor(y_all[:, t, :], fw[:, q], y_all[:, t, :], ALU.add).then_inc(f_sum, 1)

            for q in range(4):
                values(q, q, first_four)
            residual(0, 0, 0)
            with pool.Fori(1, NT // 4) as i:
                for q in range(4):
                    values(i * 4 + q, q, i)
                    residual(i * 4 + q - 3, (q - 3) % 4, i - (q < 3))
            for t in range(NT - 3, NT):
                residual(t, t % 4, NT // 4 - 1)


_INS = ['x', 'adj', 'L0_gnn_W', 'L0_gnn_a1', 'L0_gnn_a2']
_OUTS = [((6144, 512), 'float32')]


def kernel(**inputs):
    import numpy as _np
    import concourse.bacc as _bacc
    from concourse import mybir as _mybir
    from concourse.bass_utils import run_bass_kernel_spmd as _run

    nc = _bacc.Bacc("TRN2", target_bir_lowering=False, num_devices=1)
    arrays, args = {}, []
    for name in _INS:
        a = _np.ascontiguousarray(inputs[name])
        arrays[f"in_{name}_dram"] = a
        args.append(nc.dram_tensor(f"in_{name}_dram", a.shape, _mybir.dt.from_np(a.dtype), kind="ExternalInput").ap())
    for i, (shape, dtype) in enumerate(_OUTS):
        dt = _mybir.dt.from_np(_np.dtype(dtype))
        args.append(nc.dram_tensor(f"out_{i}_dram", shape, dt, kind="ExternalOutput").ap())
    bass_gat(nc, *args)
    r = _run(nc, [arrays], core_ids=[0])
    got = tuple(r.results[0][f"out_{i}_dram"] for i in range(len(_OUTS)))
    return got[0]
```

```python
from contextlib import ExitStack

import concourse.bass as bass
from concourse import mybir

P = 128
F32, F16, BF16, F8 = mybir.dt.float32, mybir.dt.float16, mybir.dt.bfloat16, mybir.dt.float8e4
I32, I8, U8 = mybir.dt.int32, mybir.dt.int8, mybir.dt.uint8
ALU, ACT, AX = mybir.AluOpType, mybir.ActivationFunctionType, mybir.AxisListType
RMAX = bass.bass_isa.ReduceOp.max

ONE_F8 = 0x38
SLOPE = 0.2
EPS = 1e-5
VSCALE = 512.0
LEAST = 2.0 ** -22
SEG_DVE = 2
LO = 2048.0
IBT = 8
SEG = 8
RING = 4
PAIR = 2


def bass_gat(nc, x, adj, W, a1, a2, out):
    N, K = x.shape
    NH, _, D = W.shape
    NT = N // P
    KC = K // P
    IB = IBT * P
    NB = N // IB
    NG = NH // 2
    NPAIR = NT // PAIR
    NSEG = NT // SEG
    PPS = SEG // PAIR
    D1 = D + 1
    REG = 2 * D1
    PER_BANK = 512 // REG
    NACC = 2 * IBT
    NBANK = -(-NACC // PER_BANK)
    XPB = NBANK

    def acc_of(sg, t):
        return sg * IBT + t

    assert NBANK + 2 <= 8 and PPS == RING and NT % SEG == 0 and N % IB == 0

    adjt_d = nc.dram_tensor("adjt_scratch", [NB * NT // PAIR, P, PAIR, IB], U8, kind="Internal").ap()
    h_d = nc.dram_tensor("h_scratch", [N, NH * D], F32, kind="Internal").ap()
    s1_d = nc.dram_tensor("negs1_scratch", [NH * NT, P], F32, kind="Internal").ap()
    att_d = nc.dram_tensor("att_scratch", [N, NH * D1], F32, kind="Internal").ap()

    ctx = ExitStack()
    with ctx:
        def sb(name, shape, dt):
            return ctx.enter_context(nc.sbuf_tensor(name, shape, dt))

        def sem(name):
            return ctx.enter_context(nc.semaphore(name))

        ps = ctx.enter_context(nc.psum_tensor("ps", [P, 8, 512], F32))

        ADJB = NT * IB
        VB = 2 * NT * 2 * REG * 2
        big = sb("big", [P, ADJB + VB], U8)
        adjt = big[:, 0:ADJB].rearrange("p (c i) -> p c i", c=NT)
        V = big[:, ADJB:ADJB + VB].bitcast(F16).rearrange("p (h c s r) -> p h c s r", h=2, c=NT, s=2)
        y_all = big[:, 0:NT * K * 4].bitcast(F32).rearrange("p (t f) -> p t f", t=NT)

        adj_in = sb("adj_in", [P, 2, IBT, PAIR * P], I32)
        adj_bf = sb("adj_bf", [P, 2, IBT, PAIR * P], BF16)
        adj_u8 = sb("adj_u8", [P, 4, IB], U8)
        s1b = sb("s1b", [P, 2, IB], F32)
        cmp = sb("cmp", [P, RING, PAIR * IB], I8)
        pos = sb("pos", [P, RING, PAIR * IB], U8)
        neg = sb("neg", [P, RING, PAIR * IB], U8)
        raw = sb("raw", [P, NACC * REG], F32)
        comb = sb("comb", [P, NACC * D1], F32)
        num = sb("num", [P, IBT * D1], F32)
        hseg = sb("hseg", [P, 2, SEG, D1], F32)
        vtmp = sb("vtmp", [P, 2, SEG * D1], F32)
        ltmp = sb("ltmp", [P, 2, SEG * D1], F32)
        sc = sb("sc", [P, 2 * NH, NT], F32)
        negs = sb("negs", [P, 2 * NH, NT], F32)
        bd = sb("bd", [P, 2, NH, NT], F32)
        ac = sb("ac", [P, NH, 2, NT], F32)
        t1 = sb("t1", [P, NH, NT], F32)
        t2 = sb("t2", [P, NH, NT], F32)
        t3 = sb("t3", [P, NH, NT], F32)
        u = sb("u", [P, NH, NT], F32)
        cmax = sb("cmax", [P, NH], F32)
        call = sb("call", [P, NH], F32)
        hmax = sb("hmax", [P, NT], F32)
        hm = sb("hm", [P, 2], F32)
        okt = sb("okt", [P, NT, NH], F32)
        id32 = sb("id32", [P, P], F32)
        id16 = sb("id16", [P, P], BF16)
        zero16 = sb("zero16", [P, P], F16)
        s1r = sb("s1r", [P, NH * NT], F32)
        stats = sb("stats", [P, 4, 6], F32)
        mvs = sb("mvs", [P, 4, 2], F32)
        mv = sb("mv", [P, NT, 2], F32)
        std = sb("std", [P, NT], F32)
        rstd = sb("rstd", [P, NT], F32)
        epsc = sb("epsc", [P, 1], F32)
        frec = sb("frec", [P, 4, NH], F32)
        xs = cmp[:, :, :].rearrange("p a b -> p (a b)").bitcast(F32).rearrange("p (a f) -> p a f", f=K)
        hsb = pos[:, :, :].rearrange("p a b -> p (a b)").bitcast(F32).rearrange("p (a f) -> p a f", f=K)
        xT = neg[:, :, :].rearrange("p a b -> p (a b)").bitcast(F32).rearrange("p (a f) -> p a f", f=K)
        junk = big[:, ADJB + 24 * 1024:ADJB + 26 * 1024 + 0].bitcast(F32)
        hsegd = raw[:, 0:2 * SEG * D1].rearrange("p (a c f) -> p a c f", a=2, c=SEG)
        vtmpd = raw[:, 2 * SEG * D1:3 * SEG * D1]
        ltmpd = raw[:, 3 * SEG * D1:4 * SEG * D1]
        fin = adj_in[:, :, :, :].rearrange("p a t j -> p (a t j)").bitcast(F32)
        fatt = fin[:, 0:4 * NH * D1].rearrange("p (a h f) -> p a h f", a=4, h=NH)

        def f32_ring(t, pattern):
            return t.rearrange(pattern).bitcast(F32).rearrange("p (a f) -> p a f", f=K)
        fv, fr, fw = (f32_ring(m[:, :, :], "p a b -> p (a b)") for m in (cmp, pos, neg))
        fn = f32_ring(adj_bf[:, :, :, :], "p a t j -> p (a t j)")
        Wsb = big[:, ADJB:ADJB + KC * K * 4].bitcast(F32).rearrange("p (c n) -> p c n", c=KC)
        o_w = ADJB + KC * K * 4
        Wa = big[:, o_w:o_w + KC * 2 * NH * 4].bitcast(F32).rearrange("p (c n) -> p c n", c=KC)
        o_w += KC * 2 * NH * 4
        av = big[:, o_w:o_w + 2 * K * 4].bitcast(F32).rearrange("p (s n) -> p s n", s=2)
        o_w += 2 * K * 4
        wprod = big[:, o_w:o_w + 2 * KC * K * 4].bitcast(F32).rearrange("p (s c n) -> p s c n", s=2, c=KC)

        w_loaded = sem("w_loaded")
        ident_made = sem("ident_made")
        wa_step = sem("wa_step")
        x_loaded = [sem("x_loaded0"), sem("x_loaded1")]
        x_turned = sem("x_turned")
        xt_ready = sem("xt_ready")
        h_ready = sem("h_ready")
        h_copied = sem("h_copied")
        h_stored = [sem("h_stored0"), sem("h_stored1")]
        h_maxed = sem("h_maxed")
        h_sq = sem("h_sq")
        f_aggr = sem("f_aggr")
        c_part = sem("c_part")
        c_all = sem("c_all")
        tab_dve = sem("tab_dve")
        tab_act = sem("tab_act")
        s1_turned = sem("s1_turned")
        s1_stored = sem("s1_stored")
        adj_loaded = [sem("adj_loaded0"), sem("adj_loaded1")]
        adj_cast = sem("adj_cast")
        adj_turned = sem("adj_turned")
        adj_evac = sem("adj_evac")
        adj_stored = [sem("adj_stored0"), sem("adj_stored1")]
        adjt_loaded = sem("adjt_loaded")
        s1b_loaded = [sem("s1b_loaded0"), sem("s1b_loaded1")]
        cmp_act = sem("cmp_act")
        cmp_dve = sem("cmp_dve")
        pos_done = sem("pos_done")
        neg_done = sem("neg_done")
        pair_used = sem("pair_used")
        evac_act = sem("evac_act")
        evac_dve = sem("evac_dve")
        comb_step = sem("comb_step")
        raw_used = sem("raw_used")
        att_stored = sem("att_stored")
        hd_loaded = [sem("hd_loaded0"), sem("hd_loaded1")]
        hp_loaded = [sem("hp_loaded0"), sem("hp_loaded1")]
        vstep_dve = sem("vstep_dve")
        vstep_pool = sem("vstep_pool")
        v_built = [sem("v_built0"), sem("v_built1")]
        v_first = sem("v_first")
        fatt_loaded = [sem(f"fatt_loaded{q}") for q in range(4)]
        fx_loaded = [sem(f"fx_loaded{q}") for q in range(4)]
        f_rec = sem("f_rec")
        f_ok = sem("f_ok")
        f_val = sem("f_val")
        f_relu = sem("f_relu")
        f_exp = sem("f_exp")
        f_elu = sem("f_elu")
        f_sum = sem("f_sum")
        f_bn = sem("f_bn")
        f_group = sem("f_group")
        f_std = sem("f_std")
        f_rstd = sem("f_rstd")
        f_out = sem("f_out")
        out_stored = sem("out_stored")

        passed_pe, passed_dve, passed_pool, passed_sp = (
            sem(f"passed_{e}") for e in ("pe", "dve", "pool", "sp"))

        C_TURNED, C_HREADY, C_HCOP, C_MAX, C_CAST, C_CHUNK, C_EV = 2, 4, 2, 2, 2, 3, 2
        C_RING, C_BANK = RING, NBANK // 2
        C_CMP, C_NEG, C_DMA = 1, 1, 16

        adj_r = adj.rearrange("(b t p) j -> b p t j", t=IBT, p=P)
        x_r = x.rearrange("(t p) f -> t p f", p=P)
        out_r = out.rearrange("(t p) f -> t p f", p=P)
        att_r = att_d.rearrange("(t p) (h f) -> t p h f", p=P, h=NH)
        att_b = att_d.rearrange("(b t p) (h f) -> b h p t f", t=IBT, p=P, h=NH)
        h_r = h_d.rearrange("(t p) f -> t p f", p=P)
        h_s = h_d.rearrange("(s c p) (h f) -> s h p c f", c=SEG, p=P, h=NH)
        s1_rows = s1_d.rearrange("(h b t) p -> (h b) (t p)", h=NH, t=IBT)
        adjt_s = adjt_d.rearrange("(s m) p a i -> s p m (a i)", m=PPS)
        adjt32 = big[:, 0:ADJB].bitcast(I32)
        pos32, neg32, cmp32 = (a[:, :, :].bitcast(I32) for a in (pos, neg, cmp))
        pos8, neg8 = pos[:, :, :].bitcast(F8), neg[:, :, :].bitcast(F8)
        W32 = PAIR * IB // 4
        ACT_ONLY = {False: (0, 2), True: (0,)}
        DVE_CMP = {k: PPS - len(v) for k, v in ACT_ONLY.items()}

        block = ctx.enter_context(nc.Block())

        AHEAD = 4
        def due(t, lag):
            return not isinstance(t, int) or 0 <= t - lag < NT

        def turns(eng, turn):
            for i in range(AHEAD):
                turn(i)
            with eng.Fori(AHEAD, NT // 4) as i:
                turn(i)
            for i in range(NT // 4, NT // 4 + AHEAD):
                turn(i)

        @block.sync
        def _(sp):
            def load_unit(b, k, i):
                sp.wait_ge(adj_cast, b * NPAIR + k + 1 - 2 + C_CAST)
                sp.dma_start(adj_in[:, i], adj_r[b, :, :, bass.ds(k * (PAIR * P), PAIR * P)]
                             ).then_inc(adj_loaded[i], 16)

            def load_adjt(n, b, s, used):
                sp.wait_ge(neg_done, used + C_NEG)
                for e in range(2):
                    sp.wait_ge(adj_stored[e], (b * (NPAIR // 2) + (s + 1) * (PPS // 2)) * 16 + C_DMA)
                sp.wait_ge(adjt_loaded, n * 16)
                sp.sem_inc(passed_sp, 1)
                sp.dma_start(adjt[:, s * SEG:(s + 1) * SEG, :].rearrange("p (m a) i -> p m (a i)", a=PAIR),
                             adjt_s[b * NSEG + s]).then_inc(adjt_loaded, 16)

            def load_s1(head, b, hd, used):
                sp.wait_ge(cmp_act, used + C_CMP)
                sp.sem_inc(passed_sp, 1)
                sp.wait_ge(pos_done, used + C_RING)
                sp.sem_inc(passed_sp, 1)
                sp.dma_start(s1b[:, hd], s1_rows[head * NB + b].partition_broadcast(P)
                             ).then_inc(s1b_loaded[hd], 16)

            for c in range(KC):
                sp.dma_start(Wsb[:, c].rearrange("p (h f) -> p h f", h=NH),
                             W[:, c * P:(c + 1) * P, :].rearrange("h p f -> p h f")).then_inc(w_loaded, 16)
            for s, a in enumerate((a1, a2)):
                sp.dma_start(av[:, s], a.rearrange("h f -> (h f)").partition_broadcast(P)).then_inc(w_loaded, 16)

            def store_unit(u, e):
                sp.wait_ge(adj_evac, u * 2 + 2 + C_EV)
                sp.sem_inc(passed_sp, 1)
                sp.dma_start(adjt_d[u], adj_u8[:, 2 * e:2 * e + 2]).then_inc(adj_stored[e], 16)

            def store_h(t, j):
                sp.wait_ge(h_copied, t + 1 + C_HCOP)
                sp.dma_start(h_r[t], hsb[:, j]).then_inc(h_stored[j], 16)

            def stage1(i, first=0):
                for e in range(2):
                    for j in range(2):
                        t = i * 4 + e * 2 + j
                        sp.wait_ge(x_turned, t + 1 - 2 + C_TURNED)
                        sp.dma_start(xs[:, j], x_r[t]).then_inc(x_loaded[j], 16)
                    if first < 1 or (first == 1 and e):
                        for j in range(2):
                            store_h(i * 4 + e * 2 - 6 + j, j)
                        store_unit(i * 2 + e - 3, 1 - e)
                    load_unit(0, i * 2 + e, e)

            stage1(0, 2)
            stage1(1, 1)
            with sp.Fori(2, NT // 4) as i:
                stage1(i)
            for t in range(NT - 6, NT):
                store_h(t, t % 2)
            store_unit(NPAIR - 3, (NPAIR - 3) % 2)

            for e in range(2):
                sp.wait_ge(h_stored[e], NT // 2 * 16 + C_DMA)
            sp.wait_ge(ident_made, 1)
            for s in range(SEG_DVE):
                sp.dma_start(hsegd[:, s, :, 0:D], h_s[s, 0]).then_inc(hd_loaded[s], 16)
            sp.wait_ge(s1_stored, 16)
            load_s1(0, 0, 0, 0)
            for s in range(NSEG - 2):
                load_adjt(s, 0, s, 0)

            def iteration(g, b, nxt, T, produce, flush=False):
                if flush:
                    for u in range(NB * NPAIR - 2, NB * NPAIR):
                        store_unit(u, u % 2)
                for s in range(NSEG):
                    if produce:
                        for i in range(2):
                            load_unit(b + 1, 2 * s + i, i)
                            store_unit((b + 1) * NPAIR + 2 * s + i - 2, i)
                    if s == 1:
                        load_s1(g * 2 + 1, b, 1, T * (2 * NPAIR))
                    if s < 2:
                        load_adjt(T * NSEG + NSEG - 2 + s, b, NSEG - 2 + s, T * (2 * NPAIR))
                for s in range(NSEG):
                    if produce:
                        for i in range(2):
                            load_unit(b + 1, NPAIR // 2 + 2 * s + i, i)
                            store_unit((b + 1) * NPAIR + NPAIR // 2 + 2 * s + i - 2, i)
                    if nxt and s == 1:
                        load_s1(nxt[0] * 2, nxt[1], 0, T * (2 * NPAIR) + NPAIR)
                    if nxt and s >= 2:
                        load_adjt((T + 1) * NSEG + s - 2, nxt[1], s - 2,
                                  T * (2 * NPAIR) + NPAIR + PPS * (s - 1))

            with sp.Fori(0, NB - 1) as b:
                iteration(0, b, (0, b + 1), b, True)
            iteration(0, NB - 1, (1, 0), NB - 1, False, flush=True)
            with sp.Fori(1, NG - 1) as g:
                with sp.Fori(0, NB - 1) as b:
                    iteration(g, b, (g, b + 1), g * NB + b, False)
                iteration(g, NB - 1, (g + 1, 0), g * NB + NB - 1, False)
            with sp.Fori(0, NB - 1) as b:
                iteration(NG - 1, b, (NG - 1, b + 1), (NG - 1) * NB + b, False)
            iteration(NG - 1, NB - 1, None, NG * NB - 1, False)

            sp.wait_ge(att_stored, 16 * 2 * NG * NB)
            sp.wait_ge(pair_used, 2 * NG * NB * NPAIR + C_RING)
            sp.wait_ge(neg_done, 2 * NG * NB * NPAIR + C_NEG)

            def turn(i):
                for q in range(4):
                    t = i * 4 + q
                    if due(t, 0):
                        if not isinstance(t, int) or t >= 4:
                            sp.wait_ge(f_val, t + 1 - 4)
                            sp.wait_ge(f_ok, t + 1 - 4)
                        sp.dma_start(fatt[:, q], att_r[t]).then_inc(fatt_loaded[q], 16)
                    if due(t, 2):
                        if not isinstance(t, int) or t - 2 >= 4:
                            sp.wait_ge(f_sum, t - 2 + 1 - 4)
                        sp.dma_start(y_all[:, t - 2, :],
                                     x_r[t - 2]).then_inc(fx_loaded[(q - 2) % 4], 16)
                    if due(t, 16):
                        sp.wait_ge(f_out, t - 16 + 1)
                        sp.dma_start(out_r[t - 16], y_all[:, t - 16, :]).then_inc(out_stored, 16)
            turns(sp, turn)
            sp.wait_ge(out_stored, 16 * NT)

        @block.scalar
        def _(act):
            def evac_chunk(c4, q):
                act.wait_ge(adj_turned, c4 * 4 + q + 1 + C_CHUNK)
                if q % 2 == 0:
                    act.wait_ge(adj_stored[q // 2], c4 * 16 + C_DMA)
                act.copy(adj_u8[:, q], ps[:, XPB + q % 2].bitcast(BF16)).then_inc(adj_evac, 1)

            def stage1(i, evacs):
                for q in range(4):
                    t, j = i * 4 + q, q % 2
                    act.wait_ge(h_ready, t + 1 + C_HREADY)
                    act.wait_ge(h_stored[j], (i * 2 + q // 2) * 16 + C_DMA)
                    act.wait_ge(h_maxed, t + 1 - 2 + C_MAX)
                    act.copy(sc[:, :, t], ps[:, 4 + j, 0:2 * NH])
                    act.copy(hsb[:, j], ps[:, 2 + j]).then_inc(h_copied, 1)
                    if q < evacs:
                        evac_chunk(i, q)

            with act.Fori(0, NT // 4 - 1) as i:
                stage1(i, 4)
            stage1(NT // 4 - 1, 2)

            act.wait_ge(tab_dve, 1)
            act.activation(bd[:, 0], t1[:, :, :], ACT.Exp).then_inc(tab_act, 1)
            act.activation(bd[:, 1], t1[:, :, :], ACT.Exp, scale=SLOPE).then_inc(tab_act, 1)
            act.wait_ge(tab_dve, 3)
            act.activation(ac[:, :, 0, :], t2[:, :, :], ACT.Exp).then_inc(tab_act, 1)
            act.activation(ac[:, :, 1, :], t3[:, :, :], ACT.Exp).then_inc(tab_act, 1)
            act.wait_ge(tab_dve, 4)

            def evac_banks(H):
                act.wait_ge(pair_used, (H + 1) * NPAIR + C_RING)
                act.wait_ge(raw_used, H)
                for n in range(0, NBANK, 2):
                    w = min(PER_BANK, NACC - n * PER_BANK) * REG
                    act.copy(raw[:, n * PER_BANK * REG:n * PER_BANK * REG + w], ps[:, n, 0:w]
                             ).then_inc(evac_act, 1)

            def segment(g, hd, T, s, produce, after=None):
                for q in range(PPS):
                    pair = (T * 2 + hd) * NPAIR + s * PPS + q
                    act.wait_ge(pos_done, pair + 1 - RING + C_RING)
                    for c in range(PAIR):
                        if c == 0 or q in ACT_ONLY[produce]:
                            i = act.activation(
                                cmp[:, q, c * IB:(c + 1) * IB], s1b[:, hd], ACT.Sign,
                                bias=negs[:, NH + g * 2 + hd, bass.ds(s * SEG + q * PAIR + c, 1)])
                    i.then_inc(cmp_act, 1)
                    if after:
                        after(s, q)

            def head(g, hd, T, produce, flush=False, first=False):
                act.wait_ge(s1b_loaded[hd], T * 16 + 16)
                n4 = T * (NPAIR // 2) + hd * NSEG + NT // 4 - 1

                def after(s, q):
                    evac_chunk(n4 + s + (1 + q) // 4, (1 + q) % 4)

                def after_first(s, q):
                    if (produce and not (first and q == 0)) or (flush and hd == 0 and q < 3):
                        after(s, q)
                    if q == 2 and not first:
                        evac_banks(T * 2 + hd - 1)
                segment(g, hd, T, 0, produce, after_first)
                with act.Fori(1, NSEG) as s:
                    segment(g, hd, T, s, produce, after if produce else None)

            head(0, 0, 0, True, first=True)
            head(0, 1, 0, True)
            with act.Fori(1, NB - 1) as b:
                for hd in range(2):
                    head(0, hd, b, True)
            for hd in range(2):
                head(0, hd, NB - 1, False, flush=True)
            with act.Fori(1, NG) as g:
                with act.Fori(0, NB) as b:
                    for hd in range(2):
                        head(g, hd, g * NB + b, False)
            evac_banks(2 * NG * NB - 1)

            def turn(i):
                for q in range(4):
                    t = i * 4 + q
                    if due(t, 0):
                        act.wait_ge(f_val, t + 1)
                        if not isinstance(t, int) or t >= 4:
                            act.wait_ge(f_elu, t + 1 - 4)
                        act.activation(fn[:, q], fv[:, q], ACT.Relu, scale=-1.0).then_inc(f_relu, 1)
                        act.activation(fr[:, q], fv[:, q], ACT.Relu)
                        act.wait_ge(f_relu, t + 1)
                        act.activation(fn[:, q], fn[:, q], ACT.Exp, scale=-1.0).then_inc(f_exp, 1)
                if due(i * 4, 8):
                    act.wait_ge(f_group, i - 1)
                    act.activation(std[:, bass.ds(i * 4 - 8, 4)], mv[:, bass.ds(i * 4 - 8, 4), 1], ACT.Sqrt,
                                   bias=epsc[:, 0:1]).then_inc(f_std, 1)
            turns(act, turn)

        @block.vector
        def _(dve):
            dve.sem_inc(adj_cast, C_CAST)
            dve.sem_inc(h_maxed, C_MAX)
            dve.sem_inc(pos_done, C_RING)
            dve.sem_inc(evac_dve, C_BANK)
            dve.sem_inc(neg_done, C_NEG)

            dve.wait_ge(w_loaded, 16 * (KC + 2))
            for s in range(2):
                dve.tensor_tensor(wprod[:, s], Wsb, av[:, s:s + 1, :].to_broadcast([P, KC, NH * D]),
                                  ALU.mult).then_inc(wa_step, 1)
            for s in range(2):
                dve.wait_ge(wa_step, s + 1)
                dve.tensor_reduce(Wa[:, :, s * NH:(s + 1) * NH],
                                  wprod[:, s].rearrange("p c (h f) -> p c h f", h=NH), AX.X, ALU.add
                                  ).then_inc(wa_step, 1)

            def cast_unit(b, k, half, i):
                un = b * NPAIR + k
                dve.wait_ge(adj_loaded[i], half * 16 + 16)
                dve.wait_ge(adj_turned, un * 2 - 2 + C_CHUNK)
                dve.tensor_scalar(adj_bf[:, i], adj_in[:, i], 0.0, float(ONE_F8), ALU.is_gt, ALU.mult
                                  ).then_inc(adj_cast, 1)

            def largest(t, j):
                dve.wait_ge(h_copied, t + 1 + C_HCOP)
                dve.wait_ge(h_maxed, t + C_MAX)
                dve.sem_inc(passed_dve, 1)
                dve.tensor_tensor_reduce(junk, hsb[:, j], hsb[:, j], 1.0, 0.0, ALU.mult, ALU.max,
                                         hm[:, j:j + 1]).then_inc(h_sq, 1)
                dve.wait_ge(h_sq, t + 1)
                dve.tensor_copy(hmax[:, bass.ds(t, 1)], hm[:, j:j + 1]).then_inc(h_maxed, 1)

            def stage1(i, first=False):
                for q in range(0, 4, 2):
                    cast_unit(0, i * 2 + q // 2, i, q // 2)
                    for j in range(2):
                        t = i * 4 + q + j
                        dve.wait_ge(x_turned, t + 1 + C_TURNED)
                        dve.wait_ge(h_ready, t + 1 - 4 + C_HREADY)
                        dve.tensor_copy(xT[:, q + j], ps[:, j]).then_inc(xt_ready, 1)
                    if not first:
                        for j in range(2):
                            largest(i * 4 + q - 4 + j, j)

            dve.wait_ge(wa_step, 4)
            stage1(0, True)
            with dve.Fori(1, NT // 4) as i:
                stage1(i)
            for t in range(NT - 4, NT):
                largest(t, t % 2)

            dve.wait_ge(h_copied, NT + C_HCOP)
            dve.tensor_reduce(cmax[:, :], sc[:, NH:2 * NH, :], AX.X, ALU.max).then_inc(c_part, 1)
            dve.wait_ge(c_all, 1)
            call_b = call[:, :].unsqueeze(2).to_broadcast([P, NH, NT])
            dve.tensor_tensor(t1[:, :, :], sc[:, NH:2 * NH, :], call_b, ALU.subtract).then_inc(tab_dve, 1)
            dve.tensor_tensor(u[:, :, :], sc[:, 0:NH, :], call_b, ALU.add).then_inc(vstep_dve, 1)
            dve.wait_ge(vstep_dve, 1)
            dve.tensor_scalar(t2[:, :, :], u[:, :, :], 1.0 - SLOPE, 0.0, ALU.mult, ALU.min).then_inc(tab_dve, 1)
            dve.tensor_scalar(t3[:, :, :], u[:, :, :], SLOPE - 1.0, 0.0, ALU.mult, ALU.min).then_inc(tab_dve, 1)
            dve.tensor_scalar(negs[:, :, :], sc[:, :, :], -1.0, None, ALU.mult).then_inc(tab_dve, 1)
            dve.wait_ge(tab_act, 2)
            dve.tensor_scalar(bd[:, :, :, :], bd[:, :, :, :], VSCALE, None, ALU.mult).then_inc(tab_dve, 1)
            dve.wait_ge(s1_turned, 1)
            dve.tensor_copy(s1r[:, :], ps[:, 0, 0:NH * NT]).then_inc(tab_dve, 1)

            def build(eng, step, base, hseg_, v_, l_, hd, s, head, done):
                for sg in range(2):
                    k = base + sg * 4
                    fac = bd[:, sg, head, s * SEG:(s + 1) * SEG].unsqueeze(2).to_broadcast([P, SEG, D1])
                    v3, l3 = (a.rearrange("p (c f) -> p c f", c=SEG) for a in (v_, l_))
                    dst = V[:, hd, s * SEG:(s + 1) * SEG, sg]
                    eng.wait_ge(step, k)
                    eng.tensor_tensor(v3, hseg_, fac, ALU.mult).then_inc(step, 1)
                    eng.wait_ge(step, k + 1)
                    eng.tensor_copy(dst[:, :, 0:D1], v3).then_inc(step, 1)
                    eng.wait_ge(step, k + 2)
                    eng.tensor_tensor(l3, v3, dst[:, :, 0:D1], ALU.subtract).then_inc(step, 1)
                    eng.wait_ge(step, k + 3)
                    i = eng.tensor_scalar(dst[:, :, D1:REG], l3, LO, None, ALU.mult)
                    i.then_inc(step, 1)
                eng.wait_ge(step, base + 8)
                eng.sem_inc(done, 1)

            dve.wait_ge(tab_dve, 5)
            dve.wait_ge(h_maxed, NT + C_MAX)
            dve.wait_ge(h_ready, NT + C_HREADY)
            for s in range(SEG_DVE):
                dve.wait_ge(hd_loaded[s], 16)
                build(dve, vstep_dve, 8 * s + 1, hsegd[:, s], vtmpd, ltmpd, 0, s, 0, v_first)

            def evac_bank(n, H):
                dve.wait_ge(raw_used, H)
                w = min(PER_BANK, NACC - n * PER_BANK) * REG
                dve.tensor_copy(raw[:, n * PER_BANK * REG:n * PER_BANK * REG + w], ps[:, n, 0:w]
                                ).then_inc(evac_dve, 1)

            def evac_banks(H):
                dve.wait_ge(pair_used, (H + 1) * NPAIR + C_RING)
                for n in range(1, NBANK, 2):
                    evac_bank(n, H)

            def segment(g, hd, T, s, produce, b=None, evac=None):
                base = (T * 2 + hd) * NPAIR + s * PPS
                n = 0
                for q in range(PPS):
                    pair = base + q
                    if evac is not None and q == PPS - 1:
                        evac_banks(evac)
                    if q not in ACT_ONLY[produce]:
                        dve.wait_ge(pos_done, pair + 1 - RING + C_RING)
                        dve.tensor_scalar(cmp[:, q, IB:2 * IB], s1b[:, hd],
                                          sc[:, NH + g * 2 + hd, bass.ds(s * SEG + q * PAIR + 1, 1)],
                                          -1.0, ALU.is_lt, ALU.mult).then_inc(cmp_dve, 1)
                        n += 1
                        n4 = (T * 2 + hd) * NSEG + s
                        past = 0 if produce else (NB - 1) * 2 * NSEG * (DVE_CMP[True] - DVE_CMP[False])
                        dve.wait_ge(cmp_dve, n4 * DVE_CMP[produce] + past + n)
                    dve.wait_ge(cmp_act, pair + 1 + C_CMP)
                    dve.wait_ge(pair_used, pair + 1 - RING + C_RING)
                    a = adjt32[:, bass.ds((s * PPS + q) * W32, W32)]
                    dve.tensor_tensor(pos32[:, q], cmp32[:, q], a, ALU.bitwise_and).then_inc(pos_done, 1)
                    dve.wait_ge(pos_done, pair + 1 + C_RING)
                    dve.tensor_tensor(neg32[:, q], pos32[:, q], a, ALU.bitwise_xor).then_inc(neg_done, 1)
                    if produce and q % 2:
                        cast_unit(b + 1, hd * (NPAIR // 2) + s * 2 + q // 2,
                                  (b + 1) * (NPAIR // 2) + hd * (NPAIR // 4) + s, q // 2)

            def head(g, hd, T, produce, b=None, first=False):
                dve.wait_ge(s1b_loaded[hd], T * 16 + 16)
                if hd == 0:
                    dve.wait_ge(adjt_loaded, T * (16 * NSEG) + 16)
                segment(g, hd, T, 0, produce, b, None if first else T * 2 + hd - 1)
                with dve.Fori(1, NSEG) as s:
                    if hd == 0:
                        dve.wait_ge(adjt_loaded, (T * NSEG + s) * 16 + 16)
                    segment(g, hd, T, s, produce, b)

            head(0, 0, 0, True, 0, first=True)
            head(0, 1, 0, True, 0)
            with dve.Fori(1, NB - 1) as b:
                for hd in range(2):
                    head(0, hd, b, True, b)
            for hd in range(2):
                head(0, hd, NB - 1, False)
            with dve.Fori(1, NG) as g:
                with dve.Fori(0, NB) as b:
                    for hd in range(2):
                        head(g, hd, g * NB + b, False)
            evac_banks(2 * NG * NB - 1)

            def turn(i):
                for q in range(4):
                    t = i * 4 + q
                    later = lambda lag: not isinstance(t, int) or t - lag >= 4
                    if due(t, 0):
                        dve.wait_ge(fatt_loaded[q], i * 16 + 16)
                        if later(0):
                            dve.wait_ge(f_val, t + 1 - 4)
                        dve.reciprocal(frec[:, q], fatt[:, q, :, D]).then_inc(f_rec, 1)
                        dve.tensor_scalar(okt[:, bass.ds(t, 1), :].rearrange("p a h -> p (a h)"),
                                          fatt[:, q, :, D], VSCALE * LEAST, None, ALU.is_ge).then_inc(f_ok, 1)
                    if due(t, 2):
                        r = (q - 2) % 4
                        dve.wait_ge(f_exp, t - 2 + 1)
                        if later(2):
                            dve.wait_ge(f_sum, t - 2 + 1 - 4)
                        dve.scalar_tensor_tensor(fw[:, r], fn[:, r], -1.0, fr[:, r], ALU.add, ALU.add
                                                 ).then_inc(f_elu, 1)
                    if due(t, 4):
                        dve.wait_ge(f_sum, t - 4 + 1)
                        if later(4):
                            dve.wait_ge(f_aggr, t - 4 + 1 - 4)
                        dve.bn_stats(stats[:, q], y_all[:, t - 4, :]).then_inc(f_bn, 1)
                    if due(t, 5):
                        r = (q - 5) % 4
                        dve.wait_ge(f_bn, t - 5 + 1)
                        if later(5):
                            dve.wait_ge(f_group, i - (1 if q else 2))
                        dve.sem_inc(passed_dve, 1)
                        dve.bn_aggr(mvs[:, r], stats[:, r]).then_inc(f_aggr, 1)
                    if q == 0 and due(t, 8):
                        dve.wait_ge(f_aggr, t - 4)
                        dve.tensor_copy(mv[:, bass.ds(t - 8, 4), :], mvs[:, :, :]).then_inc(f_group, 1)
                    if q == 0 and due(t, 12):
                        dve.wait_ge(f_std, i - 2)
                        dve.reciprocal(rstd[:, bass.ds(t - 12, 4)], std[:, bass.ds(t - 12, 4)]
                                       ).then_inc(f_rstd, 1)
                    if due(t, 12):
                        if q == 0:
                            dve.wait_ge(f_rstd, i - 2)
                        dve.tensor_scalar(y_all[:, t - 12, :], y_all[:, t - 12, :], mv[:, t - 12, 0:1],
                                          rstd[:, bass.ds(t - 12, 1)], ALU.subtract, ALU.mult
                                          ).then_inc(f_out, 1)
            turns(dve, turn)

        @block.tensor
        def _(pe):
            pe.sem_inc(x_turned, C_TURNED)
            pe.sem_inc(h_ready, C_HREADY)
            pe.sem_inc(adj_turned, C_CHUNK)
            pe.sem_inc(pair_used, C_RING)
            pe.wait_ge(ident_made, 1)

            def turn_adj(u, chunk, q):
                pe.wait_ge(adj_cast, u + 1 + C_CAST)
                pe.wait_ge(adj_evac, chunk + 1 - 2 + C_EV)
                pst = ps[:, XPB + q % 2].bitcast(BF16)
                for t in range(IBT):
                    i = pe.transpose(pst[:, t * P:(t + 1) * P],
                                     adj_bf[:, q // 2, t, q % 2 * P:(q % 2 + 1) * P], id16[:, :])
                i.then_inc(adj_turned, 1)

            def turn_x(t, j, n, first=False):
                pe.wait_ge(x_loaded[j], n * 16 + 16)
                if not first:
                    pe.wait_ge(xt_ready, t + 1 - 2)
                for c in range(KC):
                    i = pe.transpose(ps[:, j, c * P:(c + 1) * P], xs[:, j, c * P:(c + 1) * P], id32[:, :])
                i.then_inc(x_turned, 1)

            def tile_h(t, j, q):
                pe.wait_ge(xt_ready, t + 1)
                pe.wait_ge(h_copied, t + 1 - 2 + C_HCOP)
                for c in range(KC):
                    pe.matmul(ps[:, 2 + j], xT[:, q, c * P:(c + 1) * P], Wsb[:, c], start=(c == 0),
                              stop=(c == KC - 1))
                    i = pe.matmul(ps[:, 4 + j, 0:2 * NH], xT[:, q, c * P:(c + 1) * P], Wa[:, c],
                                  start=(c == 0), stop=(c == KC - 1))
                i.then_inc(h_ready, 1)

            pe.wait_ge(wa_step, 4)
            for j in range(2):
                turn_x(j, j, 0, first=True)

            def stage1(i, last=False):
                for q in range(0, 4, 2):
                    for j in range(2):
                        if not (last and q == 2):
                            turn_x(i * 4 + q + 2 + j, j, i * 2 + q // 2 + 1)
                    for j in range(2):
                        turn_adj(i * 2 + q // 2, i * 4 + q + j, q + j)
                        tile_h(i * 4 + q + j, j, q + j)

            with pe.Fori(0, NT // 4 - 1) as i:
                stage1(i)
            stage1(NT // 4 - 1, last=True)

            pe.wait_ge(tab_dve, 4)
            pe.wait_ge(xt_ready, NT)
            n1 = negs[:, 0:NH, :].rearrange("p h t -> p (h t)")
            for c in range(NH * NT // P):
                i = pe.transpose(ps[:, 0, c * P:(c + 1) * P], n1[:, c * P:(c + 1) * P], id32[:, :])
            i.then_inc(s1_turned, 1)
            pe.wait_ge(tab_dve, 6)
            pe.wait_ge(h_copied, NT + C_HCOP)

            def block_sums(g, T, produce, b=None):
                for hd in range(2):
                    H = T * 2 + hd
                    for k in range(NPAIR):
                        q = k % RING
                        if hd == 0 and k % PPS == 0 and k // PPS < SEG_DVE:
                            pe.wait_ge(v_first, k // PPS + 1)
                        if k % PPS == 0:
                            pe.wait_ge(v_built[hd], g * NSEG + k // PPS + 1)
                        for c in range(PAIR):
                            for sg, masks, done, credit in ((0, pos8, pos_done, C_RING), (1, neg8, neg_done, C_NEG)):
                                if c == 0:
                                    pe.wait_ge(done, H * NPAIR + k + 1 + credit)
                                    pe.sem_inc(passed_pe, 1)
                                for t in range(IBT):
                                    r = acc_of(sg, t)
                                    bank, off = r // PER_BANK, r % PER_BANK * REG
                                    if k == 0 and c == 0 and r % PER_BANK == 0:
                                        ev = evac_dve if bank % 2 else evac_act
                                        pe.wait_ge(ev, H * C_BANK - C_BANK + bank // 2 + 1 + C_BANK)
                                        pe.matmul(ps[:, bank, 0:2], zero16[:, :], zero16[:, 0:2], start=True,
                                                  stop=False, skip_group_check=True)
                                    i = pe.matmul(ps[:, bank, off:off + REG],
                                                  masks[:, q, c * IB + t * P:c * IB + (t + 1) * P],
                                                  V[:, hd, k * PAIR + c, sg, :], start=False,
                                                  stop=(k == NPAIR - 1 and c == PAIR - 1),
                                                  skip_group_check=True)
                        i.then_inc(pair_used, 1)
                        if produce:
                            turn_adj((b + 1) * NPAIR + hd * (NPAIR // 2) + k // 2,
                                     (b + 1) * NT + hd * NPAIR + k, k % 4)

            with pe.Fori(0, NB - 1) as b:
                block_sums(0, b, True, b)
            block_sums(0, NB - 1, False)
            with pe.Fori(1, NG) as g:
                with pe.Fori(0, NB) as b:
                    block_sums(g, g * NB + b, False)

        @block.gpsimd
        def _(pool):
            pool.sem_inc(h_copied, C_HCOP)
            pool.sem_inc(adj_evac, C_EV)
            pool.sem_inc(evac_act, C_BANK)
            pool.sem_inc(cmp_act, C_CMP)
            for d in (*h_stored, *adj_stored):
                pool.sem_inc(d, C_DMA)
            for m in (id32, id16):
                pool.memset(m[:, :], 0.0).then_inc(comb_step, 1)
            pool.wait_ge(comb_step, 2)
            for m in (id32, id16):
                pool.affine_select(out=m[:, :], in_=m[:, :], compare_op=ALU.not_equal, fill=1.0, base=0,
                                   pattern=[[-1, P]], channel_multiplier=1).then_inc(comb_step, 1)
            pool.memset(zero16[:, :], 0.0).then_inc(comb_step, 1)
            pool.memset(epsc[:, :], EPS).then_inc(comb_step, 1)
            pool.memset(hseg[:, :, :, D:D1], 1.0).then_inc(comb_step, 1)
            pool.memset(hsegd[:, :, :, D:D1], 1.0).then_inc(comb_step, 1)
            pool.sem_inc(vstep_pool, 1)
            pool.sem_inc(v_built[0], SEG_DVE)
            pool.wait_ge(comb_step, 8)
            pool.sem_inc(ident_made, 1)

            pool.wait_ge(c_part, 1)
            pool.partition_all_reduce(call[:, :], cmax[:, :], P, RMAX).then_inc(c_all, 1)
            pool.wait_ge(tab_dve, 6)
            pool.dma_start(s1_d.rearrange("(q r) p -> r q p", r=P),
                           s1r[:, :].rearrange("p (q r) -> p q r", r=P)).then_inc(s1_stored, 16)

            def load_h(m, i, head, s):
                pool.wait_ge(vstep_pool, 8 * (m - 1) + 1)
                pool.dma_start(hseg[:, i, :, 0:D], h_s[s, head]).then_inc(hp_loaded[i], 16)

            def build_segment(m, hm_, i, hd, head, s):
                pool.wait_ge(hp_loaded[i], hm_ * 16 + 16)
                for sg in range(2):
                    k = m * 8 + sg * 4 + 1
                    fac = bd[:, sg, head, s * SEG:(s + 1) * SEG].unsqueeze(2).to_broadcast([P, SEG, D1])
                    v3 = vtmp[:, sg].rearrange("p (c f) -> p c f", c=SEG)
                    l3 = ltmp[:, sg].rearrange("p (c f) -> p c f", c=SEG)
                    dst = V[:, hd, s * SEG:(s + 1) * SEG, sg]
                    pool.wait_ge(vstep_pool, k)
                    pool.tensor_tensor(v3, hseg[:, i], fac, ALU.mult).then_inc(vstep_pool, 1)
                    pool.wait_ge(vstep_pool, k + 1)
                    pool.sem_inc(passed_pool, 1)
                    pool.tensor_scalar(dst[:, :, 0:D1], v3, 1.0, 1.0, ALU.mult, ALU.mult).then_inc(vstep_pool, 1)
                    pool.wait_ge(vstep_pool, k + 2)
                    pool.tensor_tensor(l3, v3, dst[:, :, 0:D1], ALU.subtract).then_inc(vstep_pool, 1)
                    pool.wait_ge(vstep_pool, k + 3)
                    pool.sem_inc(passed_pool, 1)
                    pool.tensor_scalar(dst[:, :, D1:REG], l3, LO, 1.0, ALU.mult, ALU.mult
                                       ).then_inc(vstep_pool, 1)
                pool.wait_ge(vstep_pool, m * 8 + 8 + 1)
                pool.sem_inc(v_built[hd], 1)

            def build_first():
                todo = [(0, s) for s in range(SEG_DVE, NSEG)] + [(1, s) for s in range(NSEG)]
                for m in range(2):
                    pool.dma_start(hseg[:, m, :, 0:D], h_s[todo[m][1], todo[m][0]]).then_inc(hp_loaded[m], 16)
                for m, (hd, s) in enumerate(todo):
                    build_segment(m, m // 2, m % 2, hd, hd, s)
                    if m + 2 < len(todo):
                        load_h(m + 2, m % 2, todo[m + 2][0], todo[m + 2][1])
                return len(todo)

            def combine(g, hd, b, T):
                H = T * 2 + hd
                head = g * 2 + hd
                st = 8 + H * 4
                pool.wait_ge(evac_act, H * C_BANK + C_BANK + C_BANK)
                pool.wait_ge(evac_dve, H * C_BANK + C_BANK + C_BANK)
                r3 = raw[:, :].rearrange("p (r f) -> p r f", r=NACC)
                c3 = comb[:, :].rearrange("p (r f) -> p r f", r=NACC)
                pool.wait_ge(comb_step, st)
                pool.sem_inc(passed_pool, 1)
                pool.tensor_scalar(c3, r3[:, :, D1:REG], 1.0 / LO, 1.0, ALU.mult, ALU.mult).then_inc(comb_step, 1)
                pool.wait_ge(comb_step, st + 1)
                pool.tensor_tensor(c3, c3, r3[:, :, 0:D1], ALU.add).then_inc(comb_step, 1)
                pool.wait_ge(comb_step, st + 2)
                pool.sem_inc(raw_used, 1)
                fac = ac[:, head, :, bass.ds(b * IBT, IBT)].unsqueeze(3).to_broadcast([P, 2, IBT, D1])
                c4 = comb[:, :].rearrange("p (s t f) -> p s t f", s=2, f=D1)
                pool.tensor_tensor(c4, c4, fac, ALU.mult).then_inc(comb_step, 1)
                pool.wait_ge(comb_step, st + 3)
                pool.tensor_tensor(num[:, :].rearrange("p (t f) -> p t f", t=IBT), c4[:, 0], c4[:, 1],
                                   ALU.add).then_inc(comb_step, 1)
                pool.wait_ge(comb_step, st + 4)
                pool.dma_start(att_b[b, head], num[:, :].rearrange("p (t f) -> p t f", t=IBT)
                               ).then_inc(att_stored, 16)
                pool.wait_ge(att_stored, H * 16 + 16)

            pool.wait_ge(tab_dve, 5)
            for e in range(2):
                pool.wait_ge(h_stored[e], NT // 2 * 16 + C_DMA)
            pool.wait_ge(h_ready, NT + C_HREADY)
            pool.wait_ge(h_maxed, NT + C_MAX)
            NFIRST = build_first()
            pool.wait_ge(tab_act, 4)

            def build_next(g, hd, T):
                m0 = (g * 2 + hd) * NSEG + NFIRST
                for s in range(2):
                    load_h(m0 + s, s, g * 2 + 2 + hd, s)
                for s in range(NSEG):
                    pool.wait_ge(pair_used, (T * 2 + hd) * NPAIR + PPS * (s + 1) + C_RING)
                    build_segment(m0 + s, (g * 2 + hd) * (NSEG // 2) + NFIRST // 2 + s // 2, s % 2, hd,
                                  g * 2 + 2 + hd, s)
                    if s + 2 < NSEG:
                        load_h(m0 + s + 2, s % 2, g * 2 + 2 + hd, s + 2)

            def group(g):
                with pool.Fori(0, NB - 1) as b:
                    for hd in range(2):
                        combine(g, hd, b, g * NB + b)
                T = g * NB + NB - 1
                for hd in range(2):
                    build_next(g, hd, T)
                    combine(g, hd, NB - 1, T)

            with pool.Fori(0, NG - 1) as g:
                group(g)
            with pool.Fori(0, NB) as b:
                for hd in range(2):
                    combine(NG - 1, hd, b, (NG - 1) * NB + b)

            pool.wait_ge(neg_done, 2 * NG * NB * NPAIR + C_NEG)
            pool.wait_ge(pair_used, 2 * NG * NB * NPAIR + C_RING)

            def turn(i):
                for q in range(4):
                    t = i * 4 + q
                    if due(t, 0):
                        pool.wait_ge(f_rec, t + 1)
                        if not isinstance(t, int) or t >= 4:
                            pool.wait_ge(f_exp, t + 1 - 4)
                        pool.tensor_tensor(fv[:, q].rearrange("p (h f) -> p h f", h=NH), fatt[:, q, :, 0:D],
                                           frec[:, q].unsqueeze(2).to_broadcast([P, NH, D]), ALU.mult
                                           ).then_inc(f_val, 1)
                    if due(t, 3):
                        pool.wait_ge(f_elu, t - 3 + 1)
                        pool.wait_ge(fx_loaded[(q - 3) % 4], (i - (q < 3)) * 16 + 16)
                        pool.tensor_tensor(y_all[:, t - 3, :], fw[:, (q - 3) % 4], y_all[:, t - 3, :], ALU.add
                                           ).then_inc(f_sum, 1)
            turns(pool, turn)


_INS = ['x', 'adj', 'L0_gnn_W', 'L0_gnn_a1', 'L0_gnn_a2']
_OUTS = [((6144, 512), 'float32')]


def kernel(**inputs):
    import numpy as _np
    import concourse.bacc as _bacc
    from concourse import mybir as _mybir
    from concourse.bass_utils import run_bass_kernel_spmd as _run

    nc = _bacc.Bacc("TRN2", target_bir_lowering=False, num_devices=1)
    arrays, args = {}, []
    for name in _INS:
        a = _np.ascontiguousarray(inputs[name])
        arrays[f"in_{name}_dram"] = a
        args.append(nc.dram_tensor(f"in_{name}_dram", a.shape, _mybir.dt.from_np(a.dtype), kind="ExternalInput").ap())
    for i, (shape, dtype) in enumerate(_OUTS):
        dt = _mybir.dt.from_np(_np.dtype(dtype))
        args.append(nc.dram_tensor(f"out_{i}_dram", shape, dt, kind="ExternalOutput").ap())
    bass_gat(nc, *args)
    r = _run(nc, [arrays], core_ids=[0])
    got = tuple(r.results[0][f"out_{i}_dram"] for i in range(len(_OUTS)))
    return got[0]
```
